# Optimizing a Trainium2 kernel written in Bass

```python
import numpy as np
import jax
import jax.numpy as jnp

def _softmax(x, axis=-1):
    return jax.nn.softmax(x, axis=axis)

def _gelu(x):
    return jax.nn.gelu(x, approximate=True)

def _silu(x):
    return jax.nn.silu(x)

def _sigmoid(x):
    return jax.nn.sigmoid(x)

def _layernorm(x, axis=-1, eps=1e-05):
    m = jnp.mean(x, axis=axis, keepdims=True)
    v = jnp.var(x, axis=axis, keepdims=True)
    return (x - m) / jnp.sqrt(v + eps)

def _scatter_add(tgt, idx, src, axis=0):
    return tgt.at[idx].add(src)

def _segment_sum(src, seg, n):
    return jax.ops.segment_sum(src, seg, n)
kernel_name = 'mk_vit_tower_cls_d1_tok_img768_r4_0b9cc5'

def setup_inputs(seed: int=0):
    np.random.seed(seed)
    _w = jnp.asarray

    def _rec_inputs():
        import jax
        import jax.numpy as jnp
        _rk = jax.random.key(seed)
        x = 7.57192e-06 + 1.00007 * jax.random.normal(jax.random.fold_in(_rk, 1), (16, 3, 96, 96), jnp.float32)
        cls_tok = 0.02 * jax.random.normal(jax.random.fold_in(_rk, 5), (1, 1, 192), jnp.float32)
        return (x, cls_tok)
    x, cls_tok = _rec_inputs()

    def _L0_tok_setup():
        import jax, jax.numpy as jnp
        import numpy as np
        PATCH = 16
        HALF = PATCH // 2
        DIM = 192
        CH = 3
        PATCH_DIM = PATCH * PATCH * 5 * CH
        LN_EPS = 1e-05

        def _shift2d(x, t, l):
            H, W = (x.shape[-2], x.shape[-1])
            at, al = (abs(t), abs(l))
            xp = jnp.pad(x, ((0, 0), (0, 0), (at, at), (al, al)))
            return xp[:, :, at - t:at - t + H, al - l:al - l + W]
        key = jax.random.key(seed)
        k1, k2 = jax.random.split(key, 2)
        x = jax.random.normal(k1, (64, CH, 224, 224), dtype=jnp.float32)
        ln_gamma = jnp.ones((PATCH_DIM,), dtype=jnp.float32)
        ln_beta = jnp.zeros((PATCH_DIM,), dtype=jnp.float32)
        W = jax.random.normal(k2, (DIM, PATCH_DIM), dtype=jnp.float32) * np.float32(1.0 / np.sqrt(PATCH_DIM))
        b = jnp.zeros((DIM,), dtype=jnp.float32)
        return {'x': x, 'ln_gamma': ln_gamma, 'ln_beta': ln_beta, 'W': W, 'b': b}
    _L0_tok_all = _L0_tok_setup()
    _L0_tok_in = {k: v for k, v in _L0_tok_all.items() if k in ('ln_gamma', 'ln_beta', 'W', 'b')}
    del _L0_tok_all

    def _L0_attn_setup():
        import jax, jax.numpy as jnp
        import numpy as np
        D_MODEL = 192
        N_HEADS = 12
        HEAD_DIM = D_MODEL // N_HEADS
        THETA = 10000.0
        BATCH = 4
        SEQ = 512

        def _rope(x):
            S, D = (x.shape[-2], x.shape[-1])
            pos = jnp.arange(S, dtype=jnp.float32)
            inv_freq = THETA ** (-jnp.arange(0, D, 2, dtype=jnp.float32) / D)
            ang = pos[:, None] * inv_freq[None, :]
            cos, sin = (jnp.cos(ang), jnp.sin(ang))
            x1 = x[..., 0::2]
            x2 = x[..., 1::2]
            r1 = x1 * cos - x2 * sin
            r2 = x1 * sin + x2 * cos
            return jnp.stack([r1, r2], axis=-1).reshape(x.shape)
        key = jax.random.key(seed)
        ks = jax.random.split(key, 5)
        lim = float(np.sqrt(6.0 / (D_MODEL + D_MODEL)))

        def w(k):
            return jax.random.uniform(k, (D_MODEL, D_MODEL), jnp.float32, -lim, lim)
        return {'x': jax.random.normal(ks[0], (BATCH, SEQ, D_MODEL), jnp.float32), 'wq': w(ks[1]), 'wk': w(ks[2]), 'wv': w(ks[3]), 'wo': w(ks[4])}
    _L0_attn_all = _L0_attn_setup()
    _L0_attn_in = {k: v for k, v in _L0_attn_all.items() if k in ('wq', 'wk', 'wv', 'wo')}
    del _L0_attn_all

    def _L0_ffn_setup():
        import jax, jax.numpy as jnp
        import numpy as np
        DIM = 192
        NUM_HEADS = 12
        HEAD_DIM = DIM // NUM_HEADS
        SCALE = HEAD_DIM ** (-0.5)
        NUM_EXPERTS = 8
        RANK = 16
        ALPHA = 32
        TOPK = 2
        SCALING = ALPHA / RANK
        B, S = (8, 256)
        key = jax.random.key(seed)
        ks = jax.random.split(key, 12)
        d, e, r = (DIM, NUM_EXPERTS, RANK)
        inp = {'x': jax.random.normal(ks[0], (B, S, d), jnp.float32), 'Wg': jax.random.normal(ks[1], (e, d), jnp.float32) * 0.02, 'bg': jax.random.normal(ks[2], (e,), jnp.float32) * 0.02, 'Wqkv': jax.random.normal(ks[3], (3 * d, d), jnp.float32) * 0.02, 'bqkv': jax.random.normal(ks[4], (3 * d,), jnp.float32) * 0.02, 'Wproj': jax.random.normal(ks[5], (d, d), jnp.float32) * 0.02, 'bproj': jax.random.normal(ks[6], (d,), jnp.float32) * 0.02, 'A': jax.random.normal(ks[7], (e, r, d), jnp.float32) * 0.05, 'ba': jax.random.normal(ks[8], (e, r), jnp.float32) * 0.02, 'Bm': jax.random.normal(ks[9], (e, 3 * d, r), jnp.float32) * 0.05, 'bb': jax.random.normal(ks[10], (e, 3 * d), jnp.float32) * 0.02}
        return inp
    _L0_ffn_all = _L0_ffn_setup()
    _L0_ffn_in = {k: v for k, v in _L0_ffn_all.items() if k in ('Wg', 'bg', 'Wqkv', 'bqkv', 'Wproj', 'bproj', 'A', 'ba', 'Bm', 'bb')}
    del _L0_ffn_all
    return {'x': x, 'cls_tok': cls_tok, 'L0_tok_ln_gamma': _L0_tok_in['ln_gamma'], 'L0_tok_ln_beta': _L0_tok_in['ln_beta'], 'L0_tok_W': _L0_tok_in['W'], 'L0_tok_b': _L0_tok_in['b'], 'L0_attn_wq': _L0_attn_in['wq'], 'L0_attn_wk': _L0_attn_in['wk'], 'L0_attn_wv': _L0_attn_in['wv'], 'L0_attn_wo': _L0_attn_in['wo'], 'L0_ffn_Wg': _L0_ffn_in['Wg'], 'L0_ffn_bg': _L0_ffn_in['bg'], 'L0_ffn_Wqkv': _L0_ffn_in['Wqkv'], 'L0_ffn_bqkv': _L0_ffn_in['bqkv'], 'L0_ffn_Wproj': _L0_ffn_in['Wproj'], 'L0_ffn_bproj': _L0_ffn_in['bproj'], 'L0_ffn_A': _L0_ffn_in['A'], 'L0_ffn_ba': _L0_ffn_in['ba'], 'L0_ffn_Bm': _L0_ffn_in['Bm'], 'L0_ffn_bb': _L0_ffn_in['bb']}

def reference(x, cls_tok, L0_tok_ln_gamma, L0_tok_ln_beta, L0_tok_W, L0_tok_b, L0_attn_wq, L0_attn_wk, L0_attn_wv, L0_attn_wo, L0_ffn_Wg, L0_ffn_bg, L0_ffn_Wqkv, L0_ffn_bqkv, L0_ffn_Wproj, L0_ffn_bproj, L0_ffn_A, L0_ffn_ba, L0_ffn_Bm, L0_ffn_bb):
    import jax
    import jax.numpy as jnp

    def _L0_tok_ref(x, ln_gamma, ln_beta, W, b):
        import jax, jax.numpy as jnp
        import numpy as np
        PATCH = 16
        HALF = PATCH // 2
        DIM = 192
        CH = 3
        PATCH_DIM = PATCH * PATCH * 5 * CH
        LN_EPS = 1e-05

        def _shift2d(x, t, l):
            H, W = (x.shape[-2], x.shape[-1])
            at, al = (abs(t), abs(l))
            xp = jnp.pad(x, ((0, 0), (0, 0), (at, at), (al, al)))
            return xp[:, :, at - t:at - t + H, al - l:al - l + W]
        p = PATCH
        shifts = ((1, -1, 1, -1), (-1, 1, -1, 1), (-1, 1, 1, -1), (1, -1, -1, 1))
        parts = [x] + [_shift2d(x, HALF * s[2], HALF * s[0]) for s in shifts]
        xc = jnp.concatenate(parts, axis=1)
        B, C5, H, Wd = xc.shape
        h, w = (H // p, Wd // p)
        patches = xc.reshape(B, C5, h, p, w, p)
        patches = patches.transpose(0, 2, 4, 3, 5, 1).reshape(B, h * w, p * p * C5)
        mu = patches.mean(axis=-1, keepdims=True)
        var = patches.var(axis=-1, keepdims=True)
        xn = (patches - mu) * jax.lax.rsqrt(var + LN_EPS) * ln_gamma + ln_beta
        return jnp.einsum('bnp,dp->bnd', xn, W) + b

    def _L0_attn_ref(x, wq, wk, wv, wo):
        import jax, jax.numpy as jnp
        import numpy as np
        D_MODEL = 192
        N_HEADS = 12
        HEAD_DIM = D_MODEL // N_HEADS
        THETA = 10000.0
        BATCH = 4
        SEQ = 512

        def _rope(x):
            S, D = (x.shape[-2], x.shape[-1])
            pos = jnp.arange(S, dtype=jnp.float32)
            inv_freq = THETA ** (-jnp.arange(0, D, 2, dtype=jnp.float32) / D)
            ang = pos[:, None] * inv_freq[None, :]
            cos, sin = (jnp.cos(ang), jnp.sin(ang))
            x1 = x[..., 0::2]
            x2 = x[..., 1::2]
            r1 = x1 * cos - x2 * sin
            r2 = x1 * sin + x2 * cos
            return jnp.stack([r1, r2], axis=-1).reshape(x.shape)
        B, S, _ = x.shape
        q = (x @ wq.T).reshape(B, S, N_HEADS, HEAD_DIM).transpose(0, 2, 1, 3)
        k = (x @ wk.T).reshape(B, S, N_HEADS, HEAD_DIM).transpose(0, 2, 1, 3)
        v = (x @ wv.T).reshape(B, S, N_HEADS, HEAD_DIM).transpose(0, 2, 1, 3)
        q = _rope(q)
        k = _rope(k)
        scores = jnp.einsum('bhqd,bhkd->bhqk', q, k) / np.sqrt(HEAD_DIM).astype(np.float32)
        causal = jnp.tril(jnp.ones((S, S), dtype=bool))
        scores = jnp.where(causal, scores, -jnp.inf)
        attn = jax.nn.softmax(scores, axis=-1)
        out = jnp.einsum('bhqk,bhkd->bhqd', attn, v)
        out = out.transpose(0, 2, 1, 3).reshape(B, S, D_MODEL)
        return out @ wo.T

    def _L0_ffn_ref(x, Wg, bg, Wqkv, bqkv, Wproj, bproj, A, ba, Bm, bb):
        import jax, jax.numpy as jnp
        import numpy as np
        DIM = 192
        NUM_HEADS = 12
        HEAD_DIM = DIM // NUM_HEADS
        SCALE = HEAD_DIM ** (-0.5)
        NUM_EXPERTS = 8
        RANK = 16
        ALPHA = 32
        TOPK = 2
        SCALING = ALPHA / RANK
        B, S = (8, 256)
        b, s, d = x.shape
        t = b * s
        xf = x.reshape(t, d)
        probs = jax.nn.softmax(xf @ Wg.T + bg, axis=-1)
        top_w, top_idx = jax.lax.top_k(probs, TOPK)
        combine = jnp.zeros((t, NUM_EXPERTS), x.dtype).at[jnp.arange(t)[:, None], top_idx].add(top_w)
        h = jnp.einsum('td,erd->ter', xf, A) + ba
        hw = h * combine[:, :, None]
        delta = jnp.einsum('ter,eor->to', hw, Bm) + combine @ bb
        delta = delta * SCALING
        qkv = xf @ Wqkv.T + bqkv + delta
        qkv = qkv.reshape(b, s, 3, NUM_HEADS, HEAD_DIM)
        qkv = jnp.transpose(qkv, (2, 0, 3, 1, 4))
        q, k, v = (qkv[0], qkv[1], qkv[2])
        attn = jax.nn.softmax(jnp.einsum('bhsd,bhtd->bhst', q, k) * SCALE, axis=-1)
        out = jnp.einsum('bhst,bhtd->bhsd', attn, v)
        out = jnp.transpose(out, (0, 2, 1, 3)).reshape(b, s, d)
        return out @ Wproj.T + bproj
    h = _L0_tok_ref(x, L0_tok_ln_gamma, L0_tok_ln_beta, L0_tok_W, L0_tok_b)
    h = jnp.concatenate([jnp.broadcast_to(cls_tok, (h.shape[0], 1, h.shape[2])), h], axis=1)
    h = h + _L0_attn_ref(_layernorm(h, axis=-1), L0_attn_wq, L0_attn_wk, L0_attn_wv, L0_attn_wo)
    h = h + _L0_ffn_ref(_layernorm(h, axis=-1), L0_ffn_Wg, L0_ffn_bg, L0_ffn_Wqkv, L0_ffn_bqkv, L0_ffn_Wproj, L0_ffn_bproj, L0_ffn_A, L0_ffn_ba, L0_ffn_Bm, L0_ffn_bb)
    return h

_drawn_inputs = setup_inputs


def setup_inputs(seed=0):
    import zlib

    import numpy as np

    out = dict(_drawn_inputs(seed))
    spreads = {'L0_tok_ln_gamma': (1.0, 0.2), 'L0_tok_ln_beta': (0.0, 0.1), 'L0_tok_b': (0.0, 0.1)}
    factors = {'L0_ffn_Wg': 8.0,
     'L0_ffn_bg': 8.0,
     'L0_ffn_Wqkv': 2.749,
     'L0_ffn_bqkv': 8.0,
     'L0_ffn_bproj': 11.926,
     'L0_ffn_A': 8.0,
     'L0_ffn_ba': 8.0,
     'L0_ffn_Bm': 8.0,
     'L0_ffn_bb': 8.0}
    for name, (base, spread) in spreads.items():
        noise = np.random.default_rng([zlib.crc32(name.encode()), seed]).standard_normal(out[name].shape)
        drawn = base * np.exp(spread * noise) if base else spread * noise
        out[name] = jnp.asarray(drawn.astype(out[name].dtype))
    for name, factor in factors.items():
        out[name] = (out[name] * factor).astype(out[name].dtype)
    return out
```

```python
from contextlib import ExitStack

import concourse.bass as bass
from concourse import mybir
from concourse.alu_op_type import AluOpType as ALU

F32 = mybir.dt.float32
F32R = mybir.dt.float32r
BF16 = mybir.dt.bfloat16
U32 = mybir.dt.uint32
ACT = mybir.ActivationFunctionType
AX_X = mybir.AxisListType.X

P = 128
IMG = 16
CH = 3
GRID = 6
ROWS = 2 * GRID
WINS = GRID + 1
NPATCH = GRID * GRID
SEQ = NPATCH + 1
DIM = 192
HEADS = 12
HD = DIM // HEADS
EXP = 8
RANK = 16
TILES = IMG // 2
SLOT = 64
PDIM = 16 * 16 * 5 * CH
LN_EPS = 1e-5
LIN = DIM + EXP + 1
KB = DIM - P + EXP + 1
HALF = IMG // 2 * NPATCH
PAIR = 4 * HD
SMAX_SCALE = HD ** -0.5

C_ID = 0
C_SELW = C_ID + P
C_SELB = C_SELW + P
C_STACK = C_SELB + P
C_COS = C_STACK + 64
C_SIN = C_COS + HD
C_TOK = C_SIN + HD
C_NTOK = C_TOK + 1
C_ONE = C_NTOK + 1
C_W0 = C_ONE + 1
C_W1 = C_W0 + 1
C_SELS = C_W1 + 1
C_IOTA = C_SELS + 2
C_HALF = C_IOTA + EXP
C_MASK = C_HALF + TILES
C_N = C_MASK + 6 * SEQ

L_QKV1 = 0
L_O1 = L_QKV1 + 2 * 3 * DIM
L_QKV2 = L_O1 + 2 * DIM
L_AR = L_QKV2 + 3 * 3 * DIM
L_P2 = L_AR + 2 * (P + EXP)
L_BAR = L_P2 + 2 * DIM
L_BP = L_BAR + P + EXP
L_N = L_BP + DIM


def vit_tower(nc, x, tokw, tokgb, lnb, cls, lw, con, out):
    with ExitStack() as ctx:
        def sb(name, shape, dt=F32):
            return ctx.enter_context(nc.sbuf_tensor(name, shape, dt))

        def sem(name):
            return ctx.enter_context(nc.semaphore(name))

        xin = sb("xin", [P, CH, IMG * ROWS * WINS])
        xh = sb("xh", [P, CH, IMG * ROWS * WINS], F32R)
        xl = sb("xl", [P, CH, IMG * ROWS * WINS], F32R)
        xsum = sb("xsum", [P, IMG * ROWS * WINS])
        xsq = sb("xsq", [P, 2, IMG * ROWS * WINS])
        win = sb("win", [P, CH, 10, DIM])
        wg = sb("wg", [P, 2, 10, DIM])
        ws = sb("ws", [P, CH, 8, 3 * P], F32R)
        gb = sb("gb", [P, CH * 10, 2])
        brow = sb("brow", [1, DIM + P])
        clsT = sb("clsT", [P, 2])
        cn = sb("cn", [P, C_N])
        mk = sb("mk", [P, P + 6 * SEQ], BF16)
        lws = sb("lws", [P, L_N])
        eT = sb("eT", [P, 2, TILES, P])
        rows = sb("rows", [P, DIM])
        stT = sb("stT", [P, TILES, P])
        wsrep = sb("wsrep", [P, DIM])
        bmrep = sb("bmrep", [P, DIM])
        st = sb("st", [P, 8, TILES])
        hid = sb("hid", [P, TILES, DIM])
        hbase = sb("hbase", [P, 2, DIM])
        bns = sb("bns", [P, 2, 6])
        mv = sb("mv", [P, 2, 4])
        xn = sb("xn", [P, 2, LIN + 7])
        xT = sb("xT", [P, 2, P])
        xwT = sb("xwT", [P, P])
        hwT = sb("hwT", [P, P])
        hal = sb("hal", [P, P + EXP])
        rt = sb("rt", [P, 8, EXP])
        rti = sb("rti", [P, EXP], U32)
        hw = sb("hw", [P, P])
        rc = win[:, 0, 0:2].rearrange("p a (g d) -> p (a g) d", d=HD)
        rs = win[:, 0, 2:4].rearrange("p a (g d) -> p (a g) d", d=HD)
        qr = sb("qr", [P, 2, 24, 32])
        vs = sb("vs", [P, 2, HEADS, HD + 1])
        qT = sb("qT", [P, 2, 3, P])
        kT = sb("kT", [P, 2, 3, P])
        pr = sb("pr", [P, 6, 2, SLOT])
        mx = sb("mx", [P, HEADS])
        pT = sb("pT", [P, 6, 2, SLOT])
        rec = sb("rec", [P, 2, 6])
        on = sb("on", [P, 2, 6, HD])
        oT = sb("oT", [96, 2, P])

        bank = [ctx.enter_context(nc.psum_tensor(f"bank{i}", [P, 512], F32)) for i in range(2)]
        pt2 = ctx.enter_context(nc.psum_tensor("pt2", [P, 2, 512], F32))
        bank += [None, None] + [ctx.enter_context(nc.psum_tensor(f"bank{i}", [P, 512], F32)) for i in range(4, 8)]
        bank[2], bank[3] = pt2[:, 0, :], pt2[:, 1, :]

        ident = cn[:, C_ID:C_ID + P]
        identb = mk[:, 0:P]
        maskb = mk[:, P:P + 6 * SEQ]

        d_x = [sem(f"d_x{c}") for c in range(CH)]
        d_w = [sem(f"d_w{c}") for c in range(CH)]
        d_gb, d_cn, d_misc, d_lw, d_out = sem("d_gb"), sem("d_cn"), sem("d_misc"), sem("d_lw"), sem("d_out")
        v_fill = sem("v_fill")
        v_wg = sem("v_wg")
        v_xl = sem("v_xl")
        v_wl = sem("v_wl")
        v_rows = sem("v_rows")
        v_rep = sem("v_rep")
        v_var = sem("v_var")
        v_eT = sem("v_eT")
        v_self = sem("v_self")
        v_tok = sem("v_tok")
        v_mv = sem("v_mv")
        v_xn = sem("v_xn")
        v_rope = sem("v_rope")
        v_qr = sem("v_qr")
        v_kt = sem("v_kt")
        v_p = sem("v_p")
        v_pt = sem("v_pt")
        v_on = sem("v_on")
        v_h = sem("v_h")
        v_lg = sem("v_lg")
        v_hw = sem("v_hw")
        a_xh = sem("a_xh")
        a_wh = sem("a_wh")
        a_sq = sem("a_sq")
        a_eT = sem("a_eT")
        a_stT = sem("a_stT")
        a_xt = sem("a_xt")
        a_v = sem("a_v")
        a_qt = sem("a_qt")
        a_e = sem("a_e")
        a_pt = sem("a_pt")
        a_ot = sem("a_ot")
        a_re = sem("a_re")
        a_hw = sem("a_hw")
        g_fill = sem("g_fill")
        g_sum = sem("g_sum")
        g_rstd0 = sem("g_rstd0")
        g_rstd = sem("g_rstd")
        p_emb = sem("p_emb")
        p_rows = sem("p_rows")
        p_st = sem("p_st")
        p_sp = sem("p_sp")
        p_rep = sem("p_rep")
        p_ht = sem("p_ht")
        p_xt = sem("p_xt")
        p_qk = sem("p_qk")
        p_v = sem("p_v")
        p_qt = sem("p_qt")
        p_kt = sem("p_kt")
        p_s = sem("p_s")
        p_pt = sem("p_pt")
        p_o = sem("p_o")
        p_ot = sem("p_ot")
        p_pr = sem("p_pr")
        p_ar = sem("p_ar")
        p_hw = sem("p_hw")

        block = ctx.enter_context(nc.Block())

        UNITS = 2 * TILES

        def gv(c):
            return gb[:, 10 * c:10 * c + 10, 0:1].to_broadcast([P, 10, DIM])

        @block.sync
        def _(sp):
            sp.dma_start(gb[:], tokgb).then_inc(d_gb, 16)
            for c in range(CH):
                sp.dma_start(win[:, c], tokw[:, c]).then_inc(d_w[c], 16)
            sp.dma_start(lws[:], lw).then_inc(d_lw, 16)
            for t in range(TILES):
                sp.wait_ge(v_h, TILES + t + 1)
                sp.dma_start(out[t], hid[:, t, :]).then_inc(d_out, 16)
            sp.wait_ge(d_out, 16 * TILES)

        @block.gpsimd
        def _(pool):
            nc.gpsimd.memset(qr[:], 0.0).then_inc(g_fill, 1)
            nc.gpsimd.memset(pr[:], 0.0).then_inc(g_fill, 1)
            nc.gpsimd.memset(pT[:], 1.0).then_inc(g_fill, 1)
            nc.gpsimd.memset(vs[:], 1.0).then_inc(g_fill, 1)
            nc.gpsimd.memset(xn[:], 1.0).then_inc(g_fill, 1)
            pool.wait_ge(d_cn, 16)
            nc.gpsimd.tensor_copy(mk[:, 0:P], cn[:, C_ID:C_ID + P])
            nc.gpsimd.tensor_copy(mk[:, P:P + 6 * SEQ], cn[:, C_MASK:C_N]).then_inc(g_fill, 1)
            pool.wait_ge(d_x[0], 16)
            pool.wait_ge(d_x[1], 16)
            nc.gpsimd.tensor_tensor(xsum[:], xin[:, 0], xin[:, 1], ALU.add).then_inc(g_sum, 1)
            pool.wait_ge(a_sq, 2)
            nc.gpsimd.tensor_tensor(xsq[:, 1], xsq[:, 0], xsq[:, 1], ALU.add).then_inc(g_sum, 1)
            pool.wait_ge(d_x[2], 16)
            pool.wait_ge(g_sum, 1)
            nc.gpsimd.tensor_tensor(xsum[:], xsum[:], xin[:, 2], ALU.add).then_inc(g_sum, 1)
            pool.wait_ge(a_sq, 3)
            pool.wait_ge(g_sum, 2)
            nc.gpsimd.tensor_tensor(xsq[:, 1], xsq[:, 1], xsq[:, 0], ALU.add).then_inc(g_sum, 1)
            pool.wait_ge(v_var, 1)
            nc.gpsimd.tensor_tensor(st[:, 3, :], st[:, 2, :], cn[:, C_HALF:C_HALF + TILES], ALU.pow).then_inc(g_rstd0, 1)
            for u in range(UNITS):
                pool.wait_ge(v_mv, u + 1)
                if u >= 2:
                    pool.wait_ge(v_xn, u - 1)
                nc.gpsimd.tensor_tensor(mv[:, u % 2, 3:4], mv[:, u % 2, 2:3], cn[:, C_HALF:C_HALF + 1],
                                        ALU.pow).then_inc(g_rstd, 1)

        @block.scalar
        def _(act):
            for c in range(CH):
                act.dma_start(xin[:, c], x[:, c]).then_inc(d_x[c], 16)
                if c == 0:
                    act.dma_start(cn[:], con).then_inc(d_cn, 16)
            act.dma_start(brow[:], lnb).then_inc(d_misc, 16)
            act.dma_start(clsT[:], cls).then_inc(d_misc, 16)
            for c in range(CH):
                act.wait_ge(d_x[c], 16)
                nc.scalar.activation(xh[:, c], xin[:, c], ACT.Copy).then_inc(a_xh, 1)
                act.wait_ge(v_wg, c + 1)
                nc.scalar.activation(ws[:, c, :, 0:P], wg[:, c % 2, 0:8, 0:P], ACT.Copy)
                nc.scalar.activation(ws[:, c, :, 2 * P:2 * P + 64], wg[:, c % 2, 0:8, P:DIM], ACT.Copy).then_inc(a_wh, 1)
                if c == 2:
                    act.wait_ge(g_sum, 2)
                nc.scalar.activation(xsq[:, c % 2], xin[:, c], ACT.Square).then_inc(a_sq, 1)
            act.wait_ge(v_fill, 3)
            act.wait_ge(p_st, 1)
            for i in range(2):
                nc.scalar.activation(
                    stT[:, 4 * i:4 * i + 4, :].rearrange("p t (s q) -> p t s q", s=2)[:, :, :, 0:NPATCH],
                    bank[5 + i][:, 0:HALF].rearrange("p (t s q) -> p t s q", t=4, s=2), ACT.Copy).then_inc(a_stT, 1)
            act.wait_ge(p_emb, 1)
            for i in range(2):
                nc.scalar.activation(
                    eT[:, 0, 4 * i:4 * i + 4, :].rearrange("p t (s q) -> p t s q", s=2)[:, :, :, 0:NPATCH],
                    bank[i][:, 0:HALF].rearrange("p (t s q) -> p t s q", t=4, s=2), ACT.Copy).then_inc(a_eT, 1)

            def xt_evac(u):
                act.wait_ge(p_xt, u + 1)
                if u >= 1:
                    act.wait_ge(p_v, u)
                if u >= TILES:
                    nc.scalar.activation(xT[0:64, 1, :], bank[5][0:64, P:2 * P], ACT.Copy)
                    nc.scalar.activation(xT[:, 0, :], bank[5][:, 0:P], ACT.Copy).then_inc(a_xt, 1)
                else:
                    nc.scalar.activation(xT[0:64, 1, :], bank[5][0:64, P:2 * P], ACT.Copy)
                    nc.scalar.activation(xT[:, 0, :], bank[5][:, 0:P], ACT.Copy).then_inc(a_xt, 1)

            def router_exp(u):
                n = u - TILES
                act.wait_ge(v_lg, n + 1)
                nc.scalar.activation(rt[:, 2, :], rt[:, 1, :], ACT.Exp, accum_out=rt[:, 3, 0:1]).then_inc(a_re, 1)

            def hw_evac(u):
                n = u - TILES
                act.wait_ge(p_hw, n + 1)
                if n >= 1:
                    act.wait_ge(p_v, u)
                nc.scalar.activation(xwT[0:KB, :], bank[5][0:KB, P:2 * P], ACT.Copy)
                nc.scalar.activation(hwT[:], bank[5][:, 0:P], ACT.Copy).then_inc(a_hw, 1)

            def v_evac(u):
                act.wait_ge(g_fill, 4)
                act.wait_ge(p_v, u + 1)
                if u >= 2:
                    act.wait_ge(p_o, u - 1)
                nc.scalar.activation(vs[:, u % 2, :, 0:HD],
                                     bank[7][:, 0:DIM].rearrange("p (h d) -> p h d", d=HD), ACT.Copy).then_inc(a_v, 1)

            def qt_evac(u):
                act.wait_ge(p_qt, u + 1)
                if u >= 2:
                    act.wait_ge(p_s, u - 1)
                nc.scalar.activation(qT[:, u % 2].rearrange("p b t -> p (b t)"), bank[5][:, 0:3 * P],
                                     ACT.Copy).then_inc(a_qt, 1)

            def exps(u):
                act.wait_ge(v_p, u + 1)
                nc.scalar.activation(pr[:, :, :, 0:SEQ], pr[:, :, :, 0:SEQ], ACT.Exp, scale=SMAX_SCALE).then_inc(a_e, 1)

            def pt_evac(u):
                act.wait_ge(g_fill, 3)
                act.wait_ge(p_pt, u + 1)
                if u >= 1:
                    act.wait_ge(p_o, u)
                nc.scalar.activation(pT[:, 0:3, :, 0:SEQ],
                                     bank[2][:, 0:3 * P].rearrange("p (g s q) -> p g s q", g=3, s=2)[:, :, :, 0:SEQ],
                                     ACT.Copy).then_inc(a_pt, 1)

            def ot_evac(u):
                act.wait_ge(p_ot, u + 1)
                nc.scalar.activation(oT[:].rearrange("p s (i q) -> p i s q", i=2),
                                     bank[4][0:96, 0:2 * P].rearrange("p (i s q) -> p i s q", i=2, s=2),
                                     ACT.Copy).then_inc(a_ot, 1)

            for u in range(UNITS + 1):
                if u >= 1:
                    exps(u - 1)
                if u < UNITS:
                    xt_evac(u)
                    if u >= TILES:
                        router_exp(u)
                if u >= 1:
                    pt_evac(u - 1)
                if u < UNITS:
                    if u >= TILES:
                        hw_evac(u)
                    v_evac(u)
                    qt_evac(u)
                if u >= 1:
                    ot_evac(u - 1)

        @block.vector
        def _(dve):
            made = [0]

            def mark(ins):
                ins.then_inc(v_self, 1)
                made[0] += 1
                return made[0]

            def after(n):
                dve.wait_ge(v_self, n)

            nc.vector.memset(bank[4][:, 0:DIM], 0.0).then_inc(v_fill, 1)
            nc.vector.memset(bank[5][:, 0:HALF], 0.0)
            nc.vector.memset(bank[6][:, 0:HALF], 0.0).then_inc(v_fill, 1)
            z = mark(nc.vector.memset(stT[:], 0.0))
            nc.vector.memset(eT[:], 0.0).then_inc(v_fill, 1)
            dve.wait_ge(d_gb, 16)
            for c in range(CH):
                dve.wait_ge(d_w[c], 16)
                m = mark(nc.vector.tensor_tensor(wg[:, c % 2], win[:, c], gv(c), ALU.mult))
                after(m)
                for half in range(2):
                    lo, hi = (64, 128) if half == 0 else (0, 64)
                    ctr = wg[lo:hi, c % 2, half:4:2, :]
                    n = mark(nc.vector.tensor_tensor(ctr, ctr, wg[lo:hi, c % 2, 8:10, :], ALU.add))
                after(n)
                nc.vector.tensor_copy(rt[:, 0, 0:1], wg[:, c % 2, 0, 0:1]).then_inc(v_wg, 1)
                dve.wait_ge(a_xh, c + 1)
                nc.vector.tensor_tensor(xl[:, c], xin[:, c], xh[:, c].bitcast(F32), ALU.subtract).then_inc(v_xl, 1)
                dve.wait_ge(a_wh, c + 1)
                nc.vector.tensor_tensor(ws[:, c, :, P:2 * P], wg[:, c % 2, 0:8, 0:P],
                                        ws[:, c, :, 0:P].bitcast(F32), ALU.subtract)
                nc.vector.tensor_tensor(ws[:, c, :, 2 * P + 64:3 * P], wg[:, c % 2, 0:8, P:DIM],
                                        ws[:, c, :, 2 * P:2 * P + 64].bitcast(F32), ALU.subtract).then_inc(v_wl, 1)
            dve.wait_ge(p_rows, 1)
            nc.vector.tensor_copy(rows[:], bank[4][:, 0:DIM]).then_inc(v_rows, 1)
            dve.wait_ge(p_rep, 1)
            nc.vector.tensor_copy(wsrep[:], bank[4][:, 0:DIM])
            m_rep = mark(nc.vector.tensor_copy(bmrep[:], bank[4][:, DIM:2 * DIM]))
            dve.wait_ge(d_misc, 32)
            after(z)
            cl = eT[:].rearrange("p c t (s q) -> p c t s q", s=2)
            for k in range(2):
                nc.vector.tensor_copy(cl[:, k, :, :, NPATCH],
                                      clsT[:, k:k + 1].unsqueeze(2).to_broadcast([P, TILES, 2]))
            dve.wait_ge(p_emb, 1)
            for i in range(2):
                nc.vector.tensor_copy(cl[:, 1, 4 * i:4 * i + 4, :, 0:NPATCH],
                                      bank[2 + i][:, 0:HALF].rearrange("p (t s q) -> p t s q", t=4, s=2)).then_inc(v_eT, 1)
            dve.wait_ge(p_sp, 1)
            dve.wait_ge(d_cn, 16)
            sp_ = bank[6][:, 0:2 * TILES].rearrange("p (t k) -> p k t", k=2)
            m = mark(nc.vector.tensor_copy(st[:, 0:2, :], sp_))
            after(m)
            m = mark(nc.vector.tensor_tensor(st[:, 4, :], st[:, 0, :], st[:, 0, :], ALU.mult))
            after(m)
            m = mark(nc.vector.tensor_tensor(st[:, 5, :], st[:, 1, :], st[:, 4, :], ALU.subtract))
            after(m)
            nc.vector.tensor_scalar(st[:, 2, :], st[:, 5, :], 0.0, LN_EPS, ALU.max, ALU.add).then_inc(v_var, 1)
            dve.wait_ge(g_rstd0, 1)
            m = mark(nc.vector.tensor_scalar(st[:, 6, :], st[:, 3, :], cn[:, C_TOK:C_TOK + 1],
                                             cn[:, C_NTOK:C_NTOK + 1], ALU.mult, ALU.add))
            after(m)
            m_st = mark(nc.vector.scalar_tensor_tensor(st[:, 7, :], st[:, 0, :], -1.0, st[:, 6, :], ALU.mult, ALU.mult))
            after(m_rep)
            after(m_st)

            def token(u):
                m = mark(nc.vector.scalar_tensor_tensor(hbase[:, u % 2], wsrep[:], st[:, 7, u:u + 1], bmrep[:],
                                                        ALU.mult, ALU.add))
                dve.wait_ge(p_ht, u + 1)
                after(m)
                m = mark(nc.vector.scalar_tensor_tensor(hid[:, u, :], bank[7][:, 0:DIM], st[:, 6, u:u + 1],
                                                        hbase[:, u % 2], ALU.mult, ALU.add))
                nc.vector.tensor_copy(rt[:, 0, 1:2], st[:, 6, 0:1]).then_inc(v_tok, 1)
                after(m)

            def stats(u):
                t = u % TILES
                if u >= TILES:
                    dve.wait_ge(v_h, u - TILES + 1)
                m = mark(nc.vector.bn_stats(bns[:, u % 2, :], hid[:, t, :]))
                after(m)
                m = mark(nc.vector.bn_aggr(mv[:, u % 2, 0:2], bns[:, u % 2, :]))
                after(m)
                nc.vector.tensor_scalar(mv[:, u % 2, 2:3], mv[:, u % 2, 1:2], LN_EPS, None, ALU.add).then_inc(v_mv, 1)

            def normalise(u):
                if u == 0:
                    dve.wait_ge(g_fill, 5)
                dve.wait_ge(g_rstd, u + 1)
                if u >= 2:
                    dve.wait_ge(p_xt, u - 1)
                nc.vector.tensor_scalar(xn[:, u % 2, 0:DIM], hid[:, u % TILES, :], mv[:, u % 2, 0:1],
                                        mv[:, u % 2, 3:4], ALU.subtract, ALU.mult).then_inc(v_xn, 1)

            def rope(u):
                dve.wait_ge(g_fill, 1)
                dve.wait_ge(p_qk, u + 1)
                src = bank[6][:, 0:2 * DIM].rearrange("p (g d) -> p g d", d=HD)
                if u < TILES:
                    cos = cn[:, C_COS:C_COS + HD].unsqueeze(1).to_broadcast([P, 24, HD])
                    sin = cn[:, C_SIN:C_SIN + HD].unsqueeze(1).to_broadcast([P, 24, HD])
                    nc.vector.tensor_tensor(rc, src, cos, ALU.mult)
                    m = mark(nc.vector.tensor_tensor(rs, src, sin, ALU.mult))
                    if u >= 2:
                        dve.wait_ge(p_kt, u - 1)
                    after(m)
                    h = HD // 2
                    nc.vector.tensor_tensor(qr[:, u % 2, :, 0:h], rc[:, :, 0:h], rs[:, :, h:HD], ALU.subtract)
                    nc.vector.tensor_tensor(qr[:, u % 2, :, h:HD], rc[:, :, h:HD], rs[:, :, 0:h], ALU.add).then_inc(v_qr, 1)
                else:
                    dve.wait_ge(p_kt, u - 1)
                    nc.vector.tensor_copy(qr[:, u % 2, :, 0:HD], src).then_inc(v_qr, 1)

            def kt_evac(u):
                dve.wait_ge(p_kt, u + 1)
                if u >= 2:
                    dve.wait_ge(p_s, u - 1)
                nc.vector.tensor_copy(kT[:, u % 2].rearrange("p b t -> p (b t)"), bank[6][:, 0:3 * P]).then_inc(v_kt, 1)

            def softmax_shift(u):
                dve.wait_ge(g_fill, 2)
                dve.wait_ge(p_s, u + 1)
                if u >= 1:
                    dve.wait_ge(p_pt, u)
                for y in range(2):
                    s = bank[y][:, 0:6 * SEQ].rearrange("p (g k) -> p g k", k=SEQ)
                    m = mark(nc.vector.tensor_reduce(mx[:, 6 * y:6 * y + 6], s, AX_X, ALU.max))
                after(m)
                for y in range(2):
                    s = bank[y][:, 0:6 * SEQ].rearrange("p (g k) -> p g k", k=SEQ)
                    ins = nc.vector.tensor_tensor(
                        pr[:, 3 * y:3 * y + 3, :, 0:SEQ].rearrange("p b i k -> p (b i) k"), s,
                        mx[:, 6 * y:6 * y + 6].unsqueeze(2).to_broadcast([P, 6, SEQ]), ALU.subtract)
                ins.then_inc(v_p, 1)

            def pt_evac(u):
                dve.wait_ge(g_fill, 3)
                dve.wait_ge(p_pt, u + 1)
                if u >= 1:
                    dve.wait_ge(p_o, u)
                nc.vector.tensor_copy(pT[:, 3:6, :, 0:SEQ],
                                      bank[3][:, 0:3 * P].rearrange("p (g s q) -> p g s q", g=3, s=2)[:, :, :, 0:SEQ]
                                      ).then_inc(v_pt, 1)

            def divide(u):
                dve.wait_ge(p_o, u + 1)
                for i in range(2):
                    o = bank[i][:, 0:6 * (HD + 1)].rearrange("p (g d) -> p g d", d=HD + 1)
                    m = mark(nc.vector.reciprocal(rec[:, i, :].unsqueeze(2), o[:, :, HD:HD + 1]))
                if u >= 1:
                    dve.wait_ge(p_ot, u)
                after(m)
                for i in range(2):
                    o = bank[i][:, 0:6 * (HD + 1)].rearrange("p (g d) -> p g d", d=HD + 1)
                    ins = nc.vector.tensor_tensor(on[:, i], o[:, :, 0:HD],
                                                  rec[:, i, :].unsqueeze(2).to_broadcast([P, 6, HD]), ALU.mult)
                ins.then_inc(v_on, 1)

            def residual(u):
                t = u % TILES
                dve.wait_ge(p_pr, u + 1)
                if u >= TILES:
                    m = mark(nc.vector.tensor_tensor(hid[:, t, :], hid[:, t, :], bank[4][:, 2 * P:2 * P + DIM], ALU.add))
                    after(m)
                    nc.vector.tensor_tensor(hid[:, t, :], hid[:, t, :], lws[:, L_BP:L_BP + DIM], ALU.add).then_inc(v_h, 1)
                else:
                    nc.vector.tensor_tensor(hid[:, t, :], hid[:, t, :], bank[4][:, 2 * P:2 * P + DIM],
                                            ALU.add).then_inc(v_h, 1)

            def router(u):
                n = u - TILES
                b = u % 2
                dve.wait_ge(p_ar, n + 1)
                dve.wait_ge(d_lw, 16)
                m = mark(nc.vector.tensor_tensor(hal[:], bank[7][:, 0:P + EXP], lws[:, L_BAR:L_BAR + P + EXP], ALU.add))
                after(m)
                m = mark(nc.vector.tensor_reduce(rt[:, 0, 0:1], hal[:, P:P + EXP], AX_X, ALU.max))
                after(m)
                nc.vector.tensor_scalar(rt[:, 1, :], hal[:, P:P + EXP], rt[:, 0, 0:1], None, ALU.subtract).then_inc(v_lg, 1)
                dve.wait_ge(a_re, n + 1)
                m = mark(nc.vector.max(rt[:, 4, :], rt[:, 2, :]))
                mr = mark(nc.vector.reciprocal(rt[:, 3, 1:2], rt[:, 3, 0:1]))
                after(m)
                m = mark(nc.vector.max_index(rti[:], rt[:, 4, :], rt[:, 2, :]))
                after(m)
                m = mark(nc.vector.tensor_copy(rt[:, 5, 0:2], rti[:, 0:2]))
                after(m)
                iota = cn[:, C_IOTA:C_IOTA + EXP]
                nc.vector.tensor_scalar(rt[:, 6, :], iota, rt[:, 5, 0:1], rt[:, 4, 0:1], ALU.is_equal, ALU.mult)
                m = mark(nc.vector.tensor_scalar(rt[:, 7, :], iota, rt[:, 5, 1:2], rt[:, 4, 1:2], ALU.is_equal, ALU.mult))
                after(m)
                m = mark(nc.vector.tensor_tensor(rt[:, 6, :], rt[:, 6, :], rt[:, 7, :], ALU.add))
                after(m)
                m = mark(nc.vector.tensor_scalar(xn[:, b, DIM:DIM + EXP], rt[:, 6, :], rt[:, 3, 1:2], 2.0, ALU.mult, ALU.mult))
                after(m)
                nc.vector.tensor_tensor(hw[:].rearrange("p (e r) -> p e r", r=RANK),
                                        hal[:, 0:P].rearrange("p (e r) -> p e r", r=RANK),
                                        xn[:, b, DIM:DIM + EXP].unsqueeze(2).to_broadcast([P, EXP, RANK]),
                                        ALU.mult).then_inc(v_hw, 1)

            for u in range(UNITS + 1):
                if u < UNITS:
                    if u < TILES:
                        token(u)
                    stats(u)
                if u >= 1:
                    softmax_shift(u - 1)
                if u < UNITS:
                    normalise(u)
                if u >= 1:
                    pt_evac(u - 1)
                if u < UNITS:
                    if u >= TILES:
                        router(u)
                if u >= 1:
                    divide(u - 1)
                if u < UNITS:
                    rope(u)
                    kt_evac(u)
                if u >= 1:
                    residual(u - 1)

        @block.tensor
        def _(pe):
            xhv = xh[:].rearrange("p c (i r m) -> p c i r m", r=ROWS, m=WINS)
            xlv = xl[:].rearrange("p c (i r m) -> p c i r m", r=ROWS, m=WINS)

            def cells(a):
                i0, i1 = (1, GRID) if a == 0 else (0, GRID - 1) if a == 3 else (0, GRID)
                r0 = 2 * i0 - 1 + a
                return i0, i1, slice(r0, r0 + 2 * (i1 - i0) - 1, 2)

            def moving(v, a, half, ih):
                return v[:, 8 * ih:8 * ih + 8, cells(a)[2], half:half + GRID]

            def patches(b, a):
                i0, i1, _ = cells(a)
                return b[:, 0:HALF].rearrange("p (n i j) -> p n i j", i=GRID, j=GRID)[:, :, i0:i1, :]

            pe.wait_ge(v_fill, 1)
            pe.wait_ge(d_gb, 16)

            def row_sums(c):
                for k in range(10):
                    n = 10 * c + k
                    g = n % 4
                    mm = pe.matmul(bank[4][32 * g:32 * g + 2, 0:DIM], gb[:, n, :], win[:, c, k, :],
                                   start=(n < 4), stop=(n >= CH * 10 - 4), tile_position=(0, 32 * g))
                return mm

            for c in range(CH):
                pe.wait_ge(d_w[c], 16)
                mm = row_sums(c)
                if c == CH - 1:
                    mm.then_inc(p_rows, 1)
                pe.wait_ge(v_xl, c + 1)
                pe.wait_ge(v_wl, c + 1)
                order = [*range(8)] if c < CH - 1 else [4, 5, 6, 7, 0, 1, 2, 3]
                for k in order:
                    kind, a2, half = k // 4, (k // 2) % 2, k % 2
                    a = 1 + a2 if kind == 0 else 3 * a2
                    first, last = c == 0 and k == 0, c == CH - 1 and k == order[-1]
                    for part, v, b0 in ((0, xhv, 0), (0, xlv, 0), (1, xhv, 0), (2, xhv, 2), (2, xlv, 2)):
                        for ih in range(2):
                            opens = first and v is xhv and part != 1
                            closes = last and ((part == 1) or (part == 2 and v is xlv))
                            mm = pe.matmul(patches(bank[b0 + ih], a), ws[:, c, k, part * P:(part + 1) * P],
                                           moving(v[:, c], a, half, ih), start=opens, stop=closes)
            mm.then_inc(p_emb, 1)
            pe.wait_ge(v_fill, 2)
            pe.wait_ge(d_cn, 16)
            pe.wait_ge(g_sum, 4)
            planes = [v.rearrange("p (i r m) -> p i r m", r=ROWS, m=WINS) for v in (xsum[:], xsq[:, 1])]
            for n, a in enumerate((1, 0, 3, 2)):
                for ih in range(2):
                    for g in range(4):
                        half = g % 2
                        w = C_ONE if a in (0, 3) else C_W0 + half
                        mm = pe.matmul(patches(bank[5 + ih][32 * g:32 * g + 1, :], a), cn[:, w:w + 1],
                                       moving(planes[g // 2], a, half, ih), start=(n == 0), stop=(n == 3),
                                       tile_position=(0, 32 * g))
            mm.then_inc(p_st, 1)
            pe.wait_ge(v_rows, 1)
            pe.wait_ge(d_misc, 32)
            pe.matmul(bank[4][:, 0:DIM], cn[:, C_SELW:C_SELW + P], rows[:], start=True, stop=True)
            pe.matmul(bank[4][:, DIM:2 * DIM], cn[:, C_SELB:C_SELB + P], rows[:], start=True, stop=False)
            pe.matmul(bank[4][:, DIM:2 * DIM], brow[:, DIM:DIM + P], brow[:, 0:DIM],
                      start=False, stop=True).then_inc(p_rep, 1)
            pe.wait_ge(a_stT, 2)
            for t in range(TILES):
                mm = pe.matmul(bank[6][:, 2 * t:2 * t + 2], stT[:, t, :], cn[:, C_SELS:C_SELS + 2], start=True, stop=True)
            mm.then_inc(p_sp, 1)
            pe.wait_ge(a_eT, 2)
            pe.wait_ge(v_eT, 2)
            pe.wait_ge(d_lw, 16)

            def embed_token(u):
                if u >= 1:
                    pe.wait_ge(a_v, u)
                pe.transpose(bank[7][:, 0:P], eT[:, 0, u, :], ident)
                pe.matmul(bank[7][:, P:DIM], eT[:, 1, u, :], cn[:, C_STACK:C_STACK + 64],
                          start=True, stop=True).then_inc(p_ht, 1)

            def x_transpose(u):
                pe.wait_ge(v_xn, u + 1)
                if u >= 1:
                    pe.wait_ge(a_qt, u)
                pe.transpose(bank[5][:, 0:P], xn[:, u % 2, 0:P], ident)
                pe.transpose(bank[5][0:64, P:2 * P], xn[:, u % 2, P:DIM], ident).then_inc(p_xt, 1)

            def qkv(u):
                if u < TILES:
                    pe.wait_ge(a_xt, u + 1)
                    w = lws[:, L_QKV1:L_O1].rearrange("p (k n) -> p k n", k=2)
                    parts = [(xT[:, 0, :], w[:, 0]), (xT[0:64, 1, :], w[0:64, 1])]
                else:
                    pe.wait_ge(a_hw, u - TILES + 1)
                    w = lws[:, L_QKV2:L_AR].rearrange("p (k n) -> p k n", k=3)
                    parts = [(xT[:, 0, :], w[:, 0]), (xwT[0:KB, :], w[0:KB, 1]), (hwT[:], w[:, 2])]
                if u >= 1:
                    pe.wait_ge(v_kt, u)
                for n, (l, r) in enumerate(parts):
                    mm = pe.matmul(bank[6][:, 0:2 * DIM], l, r[:, 0:2 * DIM], start=(n == 0), stop=(n == len(parts) - 1))
                mm.then_inc(p_qk, 1)
                if u < TILES:
                    pe.wait_ge(v_tok, u + 1)
                else:
                    pe.wait_ge(v_hw, u - TILES + 1)
                for n, (l, r) in enumerate(parts):
                    mm = pe.matmul(bank[7][:, 0:DIM], l, r[:, 2 * DIM:3 * DIM], start=(n == 0), stop=(n == len(parts) - 1))
                mm.then_inc(p_v, 1)

            def low_rank(u):
                pe.wait_ge(a_xt, u + 1)
                pe.wait_ge(a_v, u)
                w = lws[:, L_AR:L_P2].rearrange("p (k n) -> p k n", k=2)
                pe.matmul(bank[7][:, 0:P + EXP], xT[:, 0, :], w[:, 0], start=True, stop=False)
                pe.matmul(bank[7][:, 0:P + EXP], xT[0:64, 1, :], w[0:64, 1], start=False, stop=True).then_inc(p_ar, 1)

            def hw_transpose(u):
                pe.wait_ge(v_hw, u - TILES + 1)
                pe.wait_ge(a_xt, u + 1)
                pe.transpose(bank[5][:, 0:P], hw[:], ident)
                pe.transpose(bank[5][0:KB, P:2 * P], xn[:, u % 2, P:LIN], ident).then_inc(p_hw, 1)

            def qk_transpose(u):
                pe.wait_ge(v_qr, u + 1)
                q = qr[:, u % 2].rearrange("p (k b g) d -> p k b (g d)", k=2, b=3)
                if u >= TILES:
                    pe.wait_ge(a_hw, u - TILES + 1)
                for b in range(3):
                    mm = pe.transpose(bank[5][:, b * P:(b + 1) * P], q[:, 0, b, :], ident)
                mm.then_inc(p_qt, 1)
                for b in range(3):
                    mm = pe.transpose(bank[6][:, b * P:(b + 1) * P], q[:, 1, b, :], ident)
                mm.then_inc(p_kt, 1)

            def scores(u):
                pe.wait_ge(a_qt, u + 1)
                pe.wait_ge(v_kt, u + 1)
                if u >= 1:
                    pe.wait_ge(v_on, u)
                else:
                    pe.wait_ge(a_eT, 2)
                masked = u < TILES
                if masked:
                    pe.wait_ge(g_fill, 6)
                    for y in range(2):
                        pe.matmul(bank[y][:, 0:6 * SEQ], identb, maskb, start=True, stop=True,
                                  skip_group_check=True)
                for b in range(3):
                    for i in range(2):
                        for r in range(4):
                            y, s = r // 2, r % 2
                            col = (2 * b + i) * SEQ
                            mm = pe.matmul(bank[y][SLOT * s:SLOT * s + SLOT, col:col + SEQ],
                                           qT[32 * r:32 * r + HD, u % 2, b, SLOT * i:SLOT * i + SLOT],
                                           kT[32 * r:32 * r + HD, u % 2, b, SLOT * i:SLOT * i + SEQ],
                                           start=not masked, stop=True,
                                           tile_position=(32 * r, SLOT * s), skip_group_check=True)
                mm.then_inc(p_s, 1)

            def p_transpose(u):
                pe.wait_ge(a_e, u + 1)
                if u >= 1:
                    pe.wait_ge(a_pt, u)
                    pe.wait_ge(v_pt, u)
                for g in range(6):
                    mm = pe.transpose(bank[2 + g // 3][:, (g % 3) * P:(g % 3) * P + P],
                                      pr[:, g].rearrange("p i k -> p (i k)"), ident)
                mm.then_inc(p_pt, 1)

            def attend(u):
                pe.wait_ge(a_pt, u + 1)
                pe.wait_ge(v_pt, u + 1)
                pe.wait_ge(a_v, u + 1)
                pe.wait_ge(v_p, u + 1)
                for g in range(6):
                    y, b = g // 3, g % 3
                    for i in range(2):
                        for s in range(2):
                            h = 4 * b + 2 * y + s
                            mm = pe.matmul(bank[i][SLOT * s:SLOT * s + SLOT, g * (HD + 1):(g + 1) * (HD + 1)],
                                           pT[SLOT * i:SLOT * i + SEQ, g, s, :],
                                           vs[SLOT * i:SLOT * i + SEQ, u % 2, h, :],
                                           start=True, stop=True, tile_position=(SLOT * i, SLOT * s))
                mm.then_inc(p_o, 1)

            def o_transpose(u):
                pe.wait_ge(v_on, u + 1)
                if u >= 1:
                    pe.wait_ge(v_h, u)
                    pe.wait_ge(a_ot, u)
                else:
                    pe.wait_ge(v_tok, 1)
                for i in range(2):
                    mm = pe.transpose(bank[4][0:96, i * P:(i + 1) * P], on[:, i].rearrange("p g d -> p (g d)"), ident)
                mm.then_inc(p_ot, 1)

            def project(u):
                pe.wait_ge(a_ot, u + 1)
                at = L_O1 if u < TILES else L_P2
                for s in range(2):
                    mm = pe.matmul(bank[4][:, 2 * P:2 * P + DIM], oT[:, s, :], lws[0:96, at + s * DIM:at + (s + 1) * DIM],
                                   start=(s == 0), stop=(s == 1))
                mm.then_inc(p_pr, 1)

            for u in range(UNITS + 1):
                if u < TILES:
                    embed_token(u)
                if u >= 1:
                    scores(u - 1)
                if u < UNITS:
                    x_transpose(u)
                    if u >= TILES:
                        low_rank(u)
                if u >= 1:
                    p_transpose(u - 1)
                if u < UNITS:
                    if u >= TILES:
                        hw_transpose(u)
                    qkv(u)
                if u >= 1:
                    attend(u - 1)
                if u < UNITS:
                    qk_transpose(u)
                if u >= 1:
                    o_transpose(u - 1)
                    project(u - 1)


def shape_constants():
    import numpy as np
    c = np.zeros((P, C_N), np.float32)
    tok = np.arange(P) % SLOT
    real = (tok < NPATCH).astype(np.float32)
    c[:, C_ID:C_ID + P] = np.eye(P)
    for g in range(4):
        c[32 * g, C_SELW:C_SELW + P] = 1
        c[32 * g + 1, C_SELB:C_SELB + P] = real
        c[32 * g, C_SELS + g // 2] = 1 / PDIM
    c[:, C_STACK:C_STACK + 64] = np.tile(np.eye(64), (2, 1))
    pos = np.where(tok < NPATCH, tok + 1, 0).astype(np.float32)
    freq = np.float32(10000.0) ** (-np.arange(0, HD, 2, dtype=np.float32) / HD)
    ang = (pos[:, None] * freq[None, :]).astype(np.float32)
    c[:, C_COS:C_COS + HD] = np.tile(np.cos(ang), (1, 2))
    c[:, C_SIN:C_SIN + HD] = np.tile(np.sin(ang), (1, 2))
    c[:, C_TOK], c[:, C_NTOK], c[:, C_ONE] = real, 1 - real, 1
    right = np.arange(P) >= 64
    c[:, C_W0], c[:, C_W1] = 1 + right, 2 - right
    c[:, C_IOTA:C_IOTA + EXP] = np.arange(EXP)
    c[:, C_HALF:C_HALF + TILES] = -0.5
    place = np.r_[np.arange(1, SEQ), 0]
    hidden = np.where(place[None, :] > place[:, None], np.float32(-1e30), np.float32(0))
    for s in range(2):
        c[SLOT * s:SLOT * s + SEQ, C_MASK:C_N] = np.tile(hidden, (1, 6))
    return c


def kernel(**inputs):
    import numpy as np
    import concourse.bacc as bacc
    from concourse.bass_utils import run_bass_kernel_spmd

    a = {k: np.asarray(v) for k, v in inputs.items()}
    x = a["x"].reshape(IMG, CH, ROWS, 8, GRID, 2, 8)
    xp = np.zeros((2, 8, 8, CH, IMG, ROWS, WINS), np.float32)
    xp[1, :, :, :, :, :, 0:GRID] = x[:, :, :, :, :, 0].transpose(3, 5, 1, 0, 2, 4)
    xp[0, :, :, :, :, :, 1:WINS] = x[:, :, :, :, :, 1].transpose(3, 5, 1, 0, 2, 4)
    xp = xp.reshape(P, CH, IMG * ROWS * WINS)

    def tok_tiles(w):
        w = w.reshape(-1, 2, 8, 16, 5, CH)
        t = np.zeros((2, 8, 8, CH, 10, w.shape[0]), np.float32)
        copy = {(0, 0): 1, (1, 1): 2, (0, 1): 3, (1, 0): 4}
        for k in range(8):
            kind, a2, half = k // 4, (k // 2) % 2, k % 2
            row = 1 + a2 if kind == 0 else 3 * a2
            s = w[:, row % 2, :, :, copy[(row // 2, half)], :].reshape(-1, 8, 2, 8, CH)
            t[:, :, :, :, k] = s.transpose(2, 1, 3, 4, 0)
        for a2 in range(2):
            s = w[:, a2, :, :, 0, :].reshape(-1, 8, 2, 8, CH).transpose(2, 1, 3, 4, 0)
            t[1, :, :, :, 8 + a2], t[0, :, :, :, 8 + a2] = s[0], s[1]
        return t.reshape(P, CH, 10, -1)

    tokw = tok_tiles(a["L0_tok_W"])
    tokgb = tok_tiles(np.stack([a["L0_tok_ln_gamma"], a["L0_tok_ln_beta"]])).reshape(P, CH * 10, 2)
    cls = np.zeros((P, 2), np.float32)
    cls[:, 0] = a["cls_tok"].reshape(DIM)[:P]
    cls[:DIM - P, 1] = a["cls_tok"].reshape(DIM)[P:]

    lnb = np.zeros((1, DIM + P), np.float32)
    lnb[0, :DIM] = a["L0_tok_b"]
    lnb[0, DIM:] = np.arange(P) % SLOT < NPATCH

    lw = np.zeros((P, L_N), np.float32)

    def put(at, w):
        n = w.shape[1]
        lw[:, at:at + n] = w[:P]
        lw[:w.shape[0] - P, at + n:at + 2 * n] = w[P:]

    halves = np.r_[np.arange(0, HD, 2), np.arange(1, HD, 2)]
    wq, wk = (a[f"L0_attn_{n}"].reshape(HEADS, HD, DIM)[:, halves].reshape(DIM, DIM) for n in ("wq", "wk"))
    put(L_QKV1, np.concatenate([wq, wk, a["L0_attn_wv"]]).T)
    wqkv = np.concatenate([a["L0_ffn_Wqkv"].T, a["L0_ffn_bb"], a["L0_ffn_bqkv"][None]])
    put(L_QKV2, wqkv)
    lw[:, L_QKV2 + 6 * DIM:L_AR] = a["L0_ffn_Bm"].transpose(0, 2, 1).reshape(EXP * RANK, 3 * DIM)
    put(L_AR, np.concatenate([a["L0_ffn_A"].reshape(EXP * RANK, DIM), a["L0_ffn_Wg"]]).T)
    for at, w in ((L_O1, a["L0_attn_wo"]), (L_P2, a["L0_ffn_Wproj"])):
        w = w.T.reshape(3, 2, 2, HD, DIM).transpose(1, 0, 3, 2, 4).reshape(96, 2 * DIM)
        lw[:96, at:at + 2 * DIM] = w
    lw[:, L_BAR:L_BAR + P] = a["L0_ffn_ba"].reshape(1, -1)
    lw[:, L_BAR + P:L_BP] = a["L0_ffn_bg"][None]
    lw[:, L_BP:L_N] = a["L0_ffn_bproj"][None]

    arrays = {"in_x": xp, "in_tokw": tokw, "in_tokgb": tokgb, "in_b": lnb, "in_cls": cls,
              "in_lw": lw, "in_con": shape_constants()}
    arrays = {k: np.ascontiguousarray(v) for k, v in arrays.items()}
    nc = bacc.Bacc("TRN2", target_bir_lowering=False, num_devices=1)
    args = [nc.dram_tensor(k, v.shape, mybir.dt.from_np(v.dtype), kind="ExternalInput").ap() for k, v in arrays.items()]
    out = nc.dram_tensor("out", (TILES, P, DIM), F32, kind="ExternalOutput").ap()
    vit_tower(nc, *args, out)
    got = run_bass_kernel_spmd(nc, [arrays], core_ids=[0]).results[0]["out"]
    got = got.reshape(IMG, SLOT, DIM)
    return np.concatenate([got[:, NPATCH:SEQ], got[:, 0:NPATCH]], axis=1)
```

```python
from contextlib import ExitStack

import concourse.bass as bass
from concourse import mybir
from concourse.alu_op_type import AluOpType as ALU

F32 = mybir.dt.float32
F32R = mybir.dt.float32r
BF16 = mybir.dt.bfloat16
U32 = mybir.dt.uint32
ACT = mybir.ActivationFunctionType
AX_X = mybir.AxisListType.X

P = 128
IMG = 16
CH = 3
GRID = 6
ROWS = 2 * GRID
WINS = GRID + 1
NPATCH = GRID * GRID
SEQ = NPATCH + 1
DIM = 192
HEADS = 12
HD = DIM // HEADS
EXP = 8
RANK = 16
TILES = IMG // 2
SLOT = 64
PDIM = 16 * 16 * 5 * CH
LN_EPS = 1e-5
LIN = DIM + EXP + 1
KB = DIM - P + EXP + 1
HALF = IMG // 2 * NPATCH
PAIR = 4 * HD
SMAX_SCALE = HD ** -0.5

C_ID = 0
C_SELW = C_ID + P
C_SELB = C_SELW + P
C_STACK = C_SELB + P
C_COS = C_STACK + 64
C_SIN = C_COS + HD
C_TOK = C_SIN + HD
C_NTOK = C_TOK + 1
C_ONE = C_NTOK + 1
C_W0 = C_ONE + 1
C_W1 = C_W0 + 1
C_SELS = C_W1 + 1
C_IOTA = C_SELS + 2
C_HALF = C_IOTA + EXP
C_MEAN = C_HALF + TILES
C_MASK = C_MEAN + 1
C_N = C_MASK + 6 * SEQ

L_QKV1 = 0
L_O1 = L_QKV1 + 2 * 3 * DIM
L_QKV2 = L_O1 + 2 * DIM
L_AR = L_QKV2 + 3 * 3 * DIM
L_P2 = L_AR + 2 * (P + EXP)
L_BAR = L_P2 + 2 * DIM
L_BP = L_BAR + P + EXP
L_N = L_BP + DIM


def vit_tower(nc, x, tokw, tokgb, lnb, cls, lw, con, out):
    with ExitStack() as ctx:
        def sb(name, shape, dt=F32):
            return ctx.enter_context(nc.sbuf_tensor(name, shape, dt))

        def sem(name):
            return ctx.enter_context(nc.semaphore(name))

        xin = sb("xin", [P, CH, IMG * ROWS * WINS])
        xh = sb("xh", [P, CH, IMG * ROWS * WINS], F32R)
        xl = sb("xl", [P, CH, IMG * ROWS * WINS], F32R)
        xsum = sb("xsum", [P, IMG * ROWS * WINS])
        xsq = sb("xsq", [P, 2, IMG * ROWS * WINS])
        win = sb("win", [P, CH, 10, DIM])
        wg = sb("wg", [P, 2, 10, DIM])
        ws = sb("ws", [P, CH, 8, 3 * P], F32R)
        gb = sb("gb", [P, CH * 10, 2])
        brow = sb("brow", [1, DIM + P])
        clsT = sb("clsT", [P, 2])
        cn = sb("cn", [P, C_N])
        mk = sb("mk", [P, P + 6 * SEQ], BF16)
        lws = sb("lws", [P, L_N])
        eT = sb("eT", [P, 2, TILES, P])
        rows = sb("rows", [P, DIM])
        wmean = sb("wmean", [P, DIM])
        stT = sb("stT", [P, TILES, P])
        bmrep = sb("bmrep", [P, DIM])
        st = sb("st", [P, 8, TILES])
        hid = sb("hid", [P, TILES, DIM])
        hbase = sb("hbase", [P, 2, DIM])
        bns = sb("bns", [P, 2, 6])
        mv = sb("mv", [P, 2, 4])
        xn = sb("xn", [P, 2, LIN + 7])
        xT = sb("xT", [P, 2, P])
        xwT = sb("xwT", [P, P])
        hwT = sb("hwT", [P, P])
        hal = sb("hal", [P, P + EXP])
        rt = sb("rt", [P, 8, EXP])
        rti = sb("rti", [P, EXP], U32)
        hw = sb("hw", [P, P])
        rc = win[:, 0, 0:2].rearrange("p a (g d) -> p (a g) d", d=HD)
        rs = win[:, 0, 2:4].rearrange("p a (g d) -> p (a g) d", d=HD)
        qr = sb("qr", [P, 2, 24, 32])
        vs = sb("vs", [P, 2, HEADS, HD + 1])
        qT = sb("qT", [P, 2, 3, P])
        kT = sb("kT", [P, 2, 3, P])
        pr = sb("pr", [P, 6, 2, SLOT])
        mx = sb("mx", [P, HEADS])
        pT = sb("pT", [P, 6, 2, SLOT])
        rec = sb("rec", [P, 2, 6])
        on = sb("on", [P, 2, 6, HD])
        oT = sb("oT", [96, 2, P])

        pso = ctx.enter_context(nc.psum_tensor("pso", [P, 2, 512], F32))
        ppt = ctx.enter_context(nc.psum_tensor("ppt", [P, 2, 512], F32))
        bank = [pso[:, 0, :], pso[:, 1, :], ppt[:, 0, :], ppt[:, 1, :]]
        bank += [ctx.enter_context(nc.psum_tensor(f"bank{i}", [P, 512], F32)) for i in range(4, 8)]

        ident = cn[:, C_ID:C_ID + P]
        identb = mk[:, 0:P]
        maskb = mk[:, P:P + 6 * SEQ]

        d_x = [sem(f"d_x{c}") for c in range(CH)]
        d_w = [sem(f"d_w{c}") for c in range(CH)]
        d_gb, d_cn, d_misc, d_lw, d_out = sem("d_gb"), sem("d_cn"), sem("d_misc"), sem("d_lw"), sem("d_out")
        v_fill = sem("v_fill")
        v_wg = sem("v_wg")
        v_xl = sem("v_xl")
        v_wl = sem("v_wl")
        v_rows = sem("v_rows")
        v_rep = sem("v_rep")
        v_var = sem("v_var")
        v_eT = sem("v_eT")
        v_rep2 = sem("v_rep2")
        v_self = sem("v_self")
        v_mv = sem("v_mv")
        v_xn = sem("v_xn")
        v_rope = sem("v_rope")
        g_qr = sem("g_qr")
        g_bias = sem("g_bias")
        a_kt = sem("a_kt")
        a_qr = sem("a_qr")
        v_p = sem("v_p")
        v_on = sem("v_on")
        v_h = sem("v_h")
        v_lg = sem("v_lg")
        v_hw = sem("v_hw")
        a_xh = sem("a_xh")
        a_wh = sem("a_wh")
        a_sq = sem("a_sq")
        a_eT = sem("a_eT")
        a_stT = sem("a_stT")
        a_xt = sem("a_xt")
        a_v = sem("a_v")
        a_qt = sem("a_qt")
        a_e = sem("a_e")
        a_pt = sem("a_pt")
        a_ot = sem("a_ot")
        a_re = sem("a_re")
        a_hw = sem("a_hw")
        g_fill = sem("g_fill")
        g_sum = sem("g_sum")
        g_rstd0 = sem("g_rstd0")
        g_rstd = sem("g_rstd")
        p_emb = sem("p_emb")
        p_rows = sem("p_rows")
        p_st = sem("p_st")
        p_sp = sem("p_sp")
        p_rep = sem("p_rep")
        p_ht = sem("p_ht")
        p_xt = sem("p_xt")
        p_qk = sem("p_qk")
        p_v = sem("p_v")
        p_qt = sem("p_qt")
        p_kt = sem("p_kt")
        p_s = sem("p_s")
        p_pt = sem("p_pt")
        p_o = sem("p_o")
        p_ot = sem("p_ot")
        p_pr = sem("p_pr")
        p_ar = sem("p_ar")
        p_hw = sem("p_hw")

        block = ctx.enter_context(nc.Block())

        UNITS = 2 * TILES

        def gv(c):
            return gb[:, 10 * c:10 * c + 10, 0:1].to_broadcast([P, 10, DIM])

        @block.sync
        def _(sp):
            sp.dma_start(gb[:], tokgb).then_inc(d_gb, 16)
            for c in range(CH):
                sp.dma_start(win[:, c], tokw[:, c]).then_inc(d_w[c], 16)
            sp.dma_start(lws[:], lw).then_inc(d_lw, 16)
            for t in range(TILES):
                sp.wait_ge(v_h, TILES + t + 1)
                sp.dma_start(out[t], hid[:, t, :]).then_inc(d_out, 16)
            sp.wait_ge(d_out, 16 * TILES)

        @block.gpsimd
        def _(pool):
            nc.gpsimd.memset(qr[:], 0.0).then_inc(g_fill, 1)
            nc.gpsimd.memset(pr[:], 0.0).then_inc(g_fill, 1)
            nc.gpsimd.memset(pT[:], 1.0).then_inc(g_fill, 1)
            nc.gpsimd.memset(vs[:], 1.0).then_inc(g_fill, 1)
            nc.gpsimd.memset(xn[:], 1.0).then_inc(g_fill, 1)
            pool.wait_ge(d_cn, 16)
            nc.gpsimd.tensor_copy(mk[:, 0:P], cn[:, C_ID:C_ID + P])
            nc.gpsimd.tensor_copy(mk[:, P:P + 6 * SEQ], cn[:, C_MASK:C_N]).then_inc(g_fill, 1)
            pool.wait_ge(d_x[0], 16)
            pool.wait_ge(d_x[1], 16)
            nc.gpsimd.tensor_tensor(xsum[:], xin[:, 0], xin[:, 1], ALU.add).then_inc(g_sum, 1)
            pool.wait_ge(a_sq, 2)
            nc.gpsimd.tensor_tensor(xsq[:, 1], xsq[:, 0], xsq[:, 1], ALU.add).then_inc(g_sum, 1)
            pool.wait_ge(d_x[2], 16)
            pool.wait_ge(g_sum, 1)
            nc.gpsimd.tensor_tensor(xsum[:], xsum[:], xin[:, 2], ALU.add).then_inc(g_sum, 1)
            pool.wait_ge(a_sq, 3)
            pool.wait_ge(g_sum, 2)
            nc.gpsimd.tensor_tensor(xsq[:, 1], xsq[:, 1], xsq[:, 0], ALU.add).then_inc(g_sum, 1)
            pool.wait_ge(v_var, 1)
            nc.gpsimd.tensor_tensor(st[:, 3, :], st[:, 2, :], cn[:, C_HALF:C_HALF + TILES], ALU.pow).then_inc(g_rstd0, 1)

            def root(u):
                pool.wait_ge(v_mv, u + 1)
                if u >= 2:
                    pool.wait_ge(v_xn, u - 1)
                nc.gpsimd.tensor_tensor(mv[:, u % 2, 3:4], mv[:, u % 2, 2:3], cn[:, C_HALF:C_HALF + 1],
                                        ALU.pow).then_inc(g_rstd, 1)

            def rotate(u):
                h = HD // 2
                pool.wait_ge(v_rope, u + 1)
                if u >= 2:
                    pool.wait_ge(p_kt, u - 1)
                nc.gpsimd.tensor_tensor(qr[:, u % 2, :, 0:h], rc[:, :, 0:h], rs[:, :, h:HD], ALU.subtract)
                nc.gpsimd.tensor_tensor(qr[:, u % 2, :, h:HD], rc[:, :, h:HD], rs[:, :, 0:h], ALU.add).then_inc(g_qr, 1)

            def add_bias(u):
                pool.wait_ge(v_xn, u + 1)
                pool.wait_ge(d_lw, 16)
                nc.gpsimd.tensor_tensor(hid[:, u % TILES, :], hid[:, u % TILES, :], lws[:, L_BP:L_BP + DIM],
                                        ALU.add).then_inc(g_bias, 1)

            for u in range(UNITS):
                if u < TILES:
                    root(u)
                if u + 1 >= TILES and u + 1 < UNITS:
                    root(u + 1)
                    add_bias(u + 1)
                if u < TILES:
                    rotate(u)

        @block.scalar
        def _(act):
            for c in range(CH):
                act.dma_start(xin[:, c], x[:, c]).then_inc(d_x[c], 16)
                if c == 0:
                    act.dma_start(cn[:], con).then_inc(d_cn, 16)
            act.dma_start(brow[:], lnb).then_inc(d_misc, 16)
            act.dma_start(clsT[:], cls).then_inc(d_misc, 16)
            for c in range(CH):
                act.wait_ge(d_x[c], 16)
                nc.scalar.activation(xh[:, c], xin[:, c], ACT.Copy).then_inc(a_xh, 1)
                act.wait_ge(v_wg, c + 1)
                nc.scalar.activation(ws[:, c, :, 0:P], wg[:, c % 2, 0:8, 0:P], ACT.Copy)
                nc.scalar.activation(ws[:, c, :, 2 * P:2 * P + 64], wg[:, c % 2, 0:8, P:DIM], ACT.Copy).then_inc(a_wh, 1)
                if c == 2:
                    act.wait_ge(g_sum, 2)
                nc.scalar.activation(xsq[:, c % 2], xin[:, c], ACT.Square).then_inc(a_sq, 1)
            act.wait_ge(v_fill, 3)
            act.wait_ge(p_st, 1)
            for i in range(2):
                nc.scalar.activation(
                    stT[:, 4 * i:4 * i + 4, :].rearrange("p t (s q) -> p t s q", s=2)[:, :, :, 0:NPATCH],
                    bank[5 + i][:, 0:HALF].rearrange("p (t s q) -> p t s q", t=4, s=2), ACT.Copy).then_inc(a_stT, 1)
            act.wait_ge(p_emb, 1)
            for i in range(2):
                nc.scalar.activation(
                    eT[:, 0, 4 * i:4 * i + 4, :].rearrange("p t (s q) -> p t s q", s=2)[:, :, :, 0:NPATCH],
                    bank[i][:, 0:HALF].rearrange("p (t s q) -> p t s q", t=4, s=2), ACT.Copy).then_inc(a_eT, 1)

            def xt_evac(u):
                act.wait_ge(p_xt, u + 1)
                if u >= 1:
                    act.wait_ge(p_v, u)
                nc.scalar.activation(xT[0:64, 1, :], bank[4][0:64, 3 * P:4 * P], ACT.Copy)
                nc.scalar.activation(xT[:, 0, :], bank[4][:, 2 * P:3 * P], ACT.Copy).then_inc(a_xt, 1)

            def router_exp(u):
                act.wait_ge(v_lg, u - TILES + 1)
                nc.scalar.activation(rt[:, 2, :], rt[:, 1, :], ACT.Exp, accum_out=rt[:, 3, 0:1]).then_inc(a_re, 1)

            def hw_evac(u):
                act.wait_ge(p_hw, u - TILES + 1)
                nc.scalar.activation(xwT[0:KB, :], bank[5][0:KB, P:2 * P], ACT.Copy)
                nc.scalar.activation(hwT[:], bank[5][:, 0:P], ACT.Copy).then_inc(a_hw, 1)

            def qr_evac(u):
                act.wait_ge(p_qk, u + 1)
                act.wait_ge(p_kt, u - 1)
                nc.scalar.activation(qr[:, u % 2, :, 0:HD], bank[6][:, 0:2 * DIM].rearrange("p (g d) -> p g d", d=HD),
                                     ACT.Copy).then_inc(a_qr, 1)

            def v_evac(u):
                act.wait_ge(g_fill, 4)
                act.wait_ge(p_v, u + 1)
                if u >= 2:
                    act.wait_ge(p_o, 2 * (u - 1))
                nc.scalar.activation(vs[:, u % 2, :, 0:HD],
                                     bank[7][:, 0:DIM].rearrange("p (h d) -> p h d", d=HD), ACT.Copy).then_inc(a_v, 1)

            def qkt_evac(u):
                act.wait_ge(p_qt, u + 1)
                if u >= 2:
                    act.wait_ge(p_s, u - 1)
                nc.scalar.activation(qT[:, u % 2].rearrange("p b t -> p (b t)"), bank[5][:, 0:3 * P],
                                     ACT.Copy).then_inc(a_qt, 1)
                act.wait_ge(p_kt, u + 1)
                nc.scalar.activation(kT[:, u % 2].rearrange("p b t -> p (b t)"), bank[6][:, 0:3 * P],
                                     ACT.Copy).then_inc(a_kt, 1)

            def exps(u):
                act.wait_ge(v_p, u + 1)
                nc.scalar.activation(pr[:, :, :, 0:SEQ], pr[:, :, :, 0:SEQ], ACT.Exp, scale=SMAX_SCALE).then_inc(a_e, 1)

            def pt_evac(u):
                act.wait_ge(g_fill, 3)
                act.wait_ge(p_pt, u + 1)
                if u >= 1:
                    act.wait_ge(p_o, 2 * u)
                nc.scalar.activation(pT[:].rearrange("p (y b) s q -> p y (b s) q", y=2)[:, :, :, 0:SEQ],
                                     ppt[:, :, 0:3 * P].rearrange("p y (g q) -> p y g q", q=SLOT)[:, :, :, 0:SEQ],
                                     ACT.Copy).then_inc(a_pt, 1)

            def ot_evac(u):
                act.wait_ge(p_ot, u + 1)
                nc.scalar.activation(oT[:].rearrange("p s (i q) -> p i s q", i=2),
                                     bank[4][0:96, 0:2 * P].rearrange("p (i s q) -> p i s q", i=2, s=2),
                                     ACT.Copy).then_inc(a_ot, 1)

            for u in range(UNITS + 2):
                a, b = u - 1, u - 2
                if TILES <= u < UNITS:
                    xt_evac(u)
                if 0 <= a < UNITS:
                    qkt_evac(a)
                if u < TILES:
                    xt_evac(u)
                if TILES <= u < UNITS:
                    router_exp(u)
                if b >= 0:
                    ot_evac(b)
                if 0 <= a < UNITS:
                    exps(a)
                if TILES <= u < UNITS:
                    hw_evac(u)
                if 0 <= a < UNITS:
                    pt_evac(a)
                if TILES <= u < UNITS:
                    qr_evac(u)
                if u < UNITS:
                    v_evac(u)

        @block.vector
        def _(dve):
            made = [0]

            def mark(ins):
                ins.then_inc(v_self, 1)
                made[0] += 1
                return made[0]

            def after(n):
                dve.wait_ge(v_self, n)

            nc.vector.memset(bank[4][:, 0:DIM], 0.0).then_inc(v_fill, 1)
            nc.vector.memset(bank[5][:, 0:HALF], 0.0)
            nc.vector.memset(bank[6][:, 0:HALF], 0.0).then_inc(v_fill, 1)
            z = mark(nc.vector.memset(stT[:], 0.0))
            nc.vector.memset(eT[:], 0.0).then_inc(v_fill, 1)
            dve.wait_ge(d_gb, 16)
            for c in range(CH):
                dve.wait_ge(d_w[c], 16)
                m = mark(nc.vector.tensor_tensor(wg[:, c % 2], win[:, c], gv(c), ALU.mult))
                after(m)
                for half in range(2):
                    lo, hi = (64, 128) if half == 0 else (0, 64)
                    ctr = wg[lo:hi, c % 2, half:4:2, :]
                    n = mark(nc.vector.tensor_tensor(ctr, ctr, wg[lo:hi, c % 2, 8:10, :], ALU.add))
                after(n)
                nc.vector.tensor_copy(rt[:, 0, 0:1], wg[:, c % 2, 0, 0:1]).then_inc(v_wg, 1)
                dve.wait_ge(a_xh, c + 1)
                nc.vector.tensor_tensor(xl[:, c], xin[:, c], xh[:, c].bitcast(F32), ALU.subtract).then_inc(v_xl, 1)
                dve.wait_ge(a_wh, c + 1)
                nc.vector.tensor_tensor(ws[:, c, :, P:2 * P], wg[:, c % 2, 0:8, 0:P],
                                        ws[:, c, :, 0:P].bitcast(F32), ALU.subtract)
                nc.vector.tensor_tensor(ws[:, c, :, 2 * P + 64:3 * P], wg[:, c % 2, 0:8, P:DIM],
                                        ws[:, c, :, 2 * P:2 * P + 64].bitcast(F32), ALU.subtract).then_inc(v_wl, 1)
            dve.wait_ge(p_rows, 1)
            nc.vector.tensor_copy(rows[:], bank[4][:, 0:DIM]).then_inc(v_rows, 1)
            dve.wait_ge(p_rep, 1)
            nc.vector.tensor_scalar(wmean[:], bank[4][:, 0:DIM], cn[:, C_MEAN:C_MEAN + 1], None, ALU.mult)
            m_rep = mark(nc.vector.tensor_copy(bmrep[:], bank[4][:, DIM:2 * DIM]))
            dve.wait_ge(d_misc, 32)
            after(z)
            cl = eT[:].rearrange("p c t (s q) -> p c t s q", s=2)
            for k in range(2):
                nc.vector.tensor_copy(cl[:, k, :, :, NPATCH],
                                      clsT[:, k:k + 1].unsqueeze(2).to_broadcast([P, TILES, 2]))
            dve.wait_ge(p_emb, 1)
            for i in range(2):
                nc.vector.tensor_copy(cl[:, 1, 4 * i:4 * i + 4, :, 0:NPATCH],
                                      bank[2 + i][:, 0:HALF].rearrange("p (t s q) -> p t s q", t=4, s=2)).then_inc(v_eT, 1)
            dve.wait_ge(p_sp, 1)
            dve.wait_ge(d_cn, 16)
            sp_ = bank[6][:, 0:2 * TILES].rearrange("p (t k) -> p k t", k=2)
            m = mark(nc.vector.tensor_copy(st[:, 0:2, :], sp_))
            after(m)
            m = mark(nc.vector.tensor_tensor(st[:, 4, :], st[:, 0, :], st[:, 0, :], ALU.mult))
            after(m)
            m = mark(nc.vector.tensor_tensor(st[:, 5, :], st[:, 1, :], st[:, 4, :], ALU.subtract))
            after(m)
            nc.vector.tensor_scalar(st[:, 2, :], st[:, 5, :], 0.0, LN_EPS, ALU.max, ALU.add).then_inc(v_var, 1)
            dve.wait_ge(g_rstd0, 1)
            m = mark(nc.vector.tensor_scalar(st[:, 6, :], st[:, 3, :], cn[:, C_TOK:C_TOK + 1],
                                             cn[:, C_NTOK:C_NTOK + 1], ALU.mult, ALU.add))
            after(m)
            after(m_rep)

            def token(u):
                dve.wait_ge(p_ht, u + 1)
                m = mark(nc.vector.scalar_tensor_tensor(hid[:, u, :], bank[4][:, 0:DIM], st[:, 6, u:u + 1],
                                                        bmrep[:], ALU.mult, ALU.add))
                after(m)

            def stats(u):
                if u >= TILES:
                    dve.wait_ge(v_h, u - TILES + 1)
                m = mark(nc.vector.bn_stats(bns[:, u % 2, :], hid[:, u % TILES, :]))
                after(m)
                m = mark(nc.vector.bn_aggr(mv[:, u % 2, 0:2], bns[:, u % 2, :]))
                after(m)
                nc.vector.tensor_scalar(mv[:, u % 2, 2:3], mv[:, u % 2, 1:2], LN_EPS, None, ALU.add).then_inc(v_mv, 1)

            def normalise(u):
                if u == 0:
                    dve.wait_ge(g_fill, 5)
                dve.wait_ge(g_rstd, u + 1)
                if u >= 2:
                    dve.wait_ge(p_xt, u - 1)
                if u >= TILES + 2:
                    dve.wait_ge(p_hw, u - TILES - 1)
                nc.vector.tensor_scalar(xn[:, u % 2, 0:DIM], hid[:, u % TILES, :], mv[:, u % 2, 0:1],
                                        mv[:, u % 2, 3:4], ALU.subtract, ALU.mult).then_inc(v_xn, 1)

            def rope(u):
                if u == 0:
                    dve.wait_ge(g_fill, 1)
                else:
                    dve.wait_ge(g_qr, u)
                dve.wait_ge(p_qk, u + 1)
                src = bank[6][:, 0:2 * DIM].rearrange("p (g d) -> p g d", d=HD)
                cos = cn[:, C_COS:C_COS + HD].unsqueeze(1).to_broadcast([P, 24, HD])
                sin = cn[:, C_SIN:C_SIN + HD].unsqueeze(1).to_broadcast([P, 24, HD])
                nc.vector.tensor_tensor(rc, src, cos, ALU.mult)
                nc.vector.tensor_tensor(rs, src, sin, ALU.mult).then_inc(v_rope, 1)

            def softmax_shift(u):
                dve.wait_ge(g_fill, 2)
                dve.wait_ge(p_s, u + 1)
                if u >= 1:
                    dve.wait_ge(p_pt, u)
                s = pso[:, :, 0:6 * SEQ].rearrange("p y (g k) -> p y g k", k=SEQ)
                m = mark(nc.vector.tensor_reduce(mx[:].rearrange("p (y g) -> p y g", y=2), s, AX_X, ALU.max))
                after(m)
                nc.vector.tensor_tensor(
                    pr[:].rearrange("p (y b) i k -> p y (b i) k", y=2)[:, :, :, 0:SEQ], s,
                    mx[:].rearrange("p (y g) -> p y g", y=2).unsqueeze(3).to_broadcast([P, 2, 6, SEQ]),
                    ALU.subtract).then_inc(v_p, 1)

            def divide(u):
                dve.wait_ge(p_o, 2 * (u + 1))
                o = ppt[:, :, 0:6 * (HD + 1)].rearrange("p i (g d) -> p i g d", d=HD + 1)
                m = mark(nc.vector.reciprocal(rec[:].unsqueeze(3), o[:, :, :, HD:HD + 1]))
                if u >= 1:
                    dve.wait_ge(p_ot, u)
                after(m)
                nc.vector.tensor_tensor(on[:], o[:, :, :, 0:HD], rec[:].unsqueeze(3).to_broadcast([P, 2, 6, HD]),
                                        ALU.mult).then_inc(v_on, 1)

            def residual(u):
                t = u % TILES
                dve.wait_ge(p_pr, u + 1)
                if u >= TILES:
                    dve.wait_ge(g_bias, u - TILES + 1)
                nc.vector.tensor_tensor(hid[:, t, :], hid[:, t, :], bank[4][:, 2 * P:2 * P + DIM],
                                        ALU.add).then_inc(v_h, 1)

            def router(u):
                n = u - TILES
                b = u % 2
                lg = hal[:, P:P + EXP]
                iota = cn[:, C_IOTA:C_IOTA + EXP]
                dve.wait_ge(p_ar, n + 1)
                dve.wait_ge(d_lw, 16)
                m = mark(nc.vector.tensor_tensor(hal[:], bank[4][:, 0:P + EXP], lws[:, L_BAR:L_BAR + P + EXP], ALU.add))
                after(m)
                m = mark(nc.vector.max(rt[:, 0, :], lg))
                after(m)
                nc.vector.tensor_scalar(rt[:, 1, :], lg, rt[:, 0, 0:1], None, ALU.subtract).then_inc(v_lg, 1)
                m = mark(nc.vector.max_index(rti[:], rt[:, 0, :], lg))
                after(m)
                m = mark(nc.vector.tensor_copy(rt[:, 5, 0:2], rti[:, 0:2]))
                after(m)
                nc.vector.tensor_scalar(rt[:, 6, :], iota, rt[:, 5, 0:1], 2.0, ALU.is_equal, ALU.mult)
                m = mark(nc.vector.tensor_scalar(rt[:, 7, :], iota, rt[:, 5, 1:2], 2.0, ALU.is_equal, ALU.mult))
                dve.wait_ge(a_re, n + 1)
                mr = mark(nc.vector.reciprocal(rt[:, 3, 1:2], rt[:, 3, 0:1]))
                after(m)
                m = mark(nc.vector.tensor_tensor(rt[:, 4, :], rt[:, 6, :], rt[:, 7, :], ALU.add))
                after(m)
                m = mark(nc.vector.scalar_tensor_tensor(xn[:, b, DIM:DIM + EXP], rt[:, 2, :], rt[:, 3, 1:2], rt[:, 4, :],
                                                        ALU.mult, ALU.mult))
                after(m)
                nc.vector.tensor_tensor(hw[:].rearrange("p (e r) -> p e r", r=RANK),
                                        hal[:, 0:P].rearrange("p (e r) -> p e r", r=RANK),
                                        xn[:, b, DIM:DIM + EXP].unsqueeze(2).to_broadcast([P, EXP, RANK]),
                                        ALU.mult).then_inc(v_hw, 1)

            for u in range(UNITS + 2):
                a, b = u - 1, u - 2
                if u < TILES:
                    token(u)
                    stats(u)
                    normalise(u)
                if b >= 0:
                    divide(b)
                if TILES <= u < UNITS:
                    router(u)
                if 0 <= a < UNITS:
                    softmax_shift(a)
                if u < TILES:
                    rope(u)
                if b >= 0:
                    residual(b)
                if TILES <= u + 1 < UNITS:
                    stats(u + 1)
                    normalise(u + 1)

        @block.tensor
        def _(pe):
            xhv = xh[:].rearrange("p c (i r m) -> p c i r m", r=ROWS, m=WINS)
            xlv = xl[:].rearrange("p c (i r m) -> p c i r m", r=ROWS, m=WINS)

            def cells(a):
                i0, i1 = (1, GRID) if a == 0 else (0, GRID - 1) if a == 3 else (0, GRID)
                r0 = 2 * i0 - 1 + a
                return i0, i1, slice(r0, r0 + 2 * (i1 - i0) - 1, 2)

            def moving(v, a, half, ih):
                return v[:, 8 * ih:8 * ih + 8, cells(a)[2], half:half + GRID]

            def patches(b, a):
                i0, i1, _ = cells(a)
                return b[:, 0:HALF].rearrange("p (n i j) -> p n i j", i=GRID, j=GRID)[:, :, i0:i1, :]

            pe.wait_ge(v_fill, 1)
            pe.wait_ge(d_gb, 16)

            def row_sums(c):
                for k in range(10):
                    n = 10 * c + k
                    g = n % 4
                    mm = pe.matmul(bank[4][32 * g:32 * g + 2, 0:DIM], gb[:, n, :], win[:, c, k, :],
                                   start=(n < 4), stop=(n >= CH * 10 - 4), tile_position=(0, 32 * g))
                return mm

            for c in range(CH):
                pe.wait_ge(d_w[c], 16)
                mm = row_sums(c)
                if c == CH - 1:
                    mm.then_inc(p_rows, 1)
                pe.wait_ge(v_xl, c + 1)
                pe.wait_ge(v_wl, c + 1)
                order = [*range(8)] if c < CH - 1 else [4, 5, 6, 7, 0, 1, 2, 3]
                for k in order:
                    kind, a2, half = k // 4, (k // 2) % 2, k % 2
                    a = 1 + a2 if kind == 0 else 3 * a2
                    first, last = c == 0 and k == 0, c == CH - 1 and k == order[-1]
                    for part, v, b0 in ((0, xhv, 0), (0, xlv, 0), (1, xhv, 0), (2, xhv, 2), (2, xlv, 2)):
                        for ih in range(2):
                            opens = first and v is xhv and part != 1
                            closes = last and ((part == 1) or (part == 2 and v is xlv))
                            mm = pe.matmul(patches(bank[b0 + ih], a), ws[:, c, k, part * P:(part + 1) * P],
                                           moving(v[:, c], a, half, ih), start=opens, stop=closes)
            mm.then_inc(p_emb, 1)
            pe.wait_ge(v_fill, 2)
            pe.wait_ge(d_cn, 16)
            pe.wait_ge(g_sum, 4)
            planes = [v.rearrange("p (i r m) -> p i r m", r=ROWS, m=WINS) for v in (xsum[:], xsq[:, 1])]
            for n, a in enumerate((1, 0, 3, 2)):
                for ih in range(2):
                    for g in range(4):
                        half = g % 2
                        w = C_ONE if a in (0, 3) else C_W0 + half
                        mm = pe.matmul(patches(bank[5 + ih][32 * g:32 * g + 1, :], a), cn[:, w:w + 1],
                                       moving(planes[g // 2], a, half, ih), start=(n == 0), stop=(n == 3),
                                       tile_position=(0, 32 * g))
            mm.then_inc(p_st, 1)
            pe.wait_ge(v_rows, 1)
            pe.wait_ge(d_misc, 32)
            pe.matmul(bank[4][:, 0:DIM], cn[:, C_SELW:C_SELW + P], rows[:], start=True, stop=True)
            pe.matmul(bank[4][:, DIM:2 * DIM], cn[:, C_SELB:C_SELB + P], rows[:], start=True, stop=False)
            pe.matmul(bank[4][:, DIM:2 * DIM], brow[:, DIM:DIM + P], brow[:, 0:DIM],
                      start=False, stop=True).then_inc(p_rep, 1)
            pe.wait_ge(a_stT, 2)
            for t in range(TILES):
                mm = pe.matmul(bank[6][:, 2 * t:2 * t + 2], stT[:, t, :], cn[:, C_SELS:C_SELS + 2], start=True, stop=True)
            mm.then_inc(p_sp, 1)
            pe.wait_ge(a_eT, 2)
            pe.wait_ge(v_eT, 2)
            pe.wait_ge(d_lw, 16)

            def embed_token(u):
                if u >= 3:
                    pe.wait_ge(v_h, u - 2)
                pe.transpose(bank[4][:, 0:P], eT[:, 0, u, :], ident)
                pe.matmul(bank[4][:, P:DIM], eT[:, 1, u, :], cn[:, C_STACK:C_STACK + 64], start=False, stop=False,
                          skip_group_check=True)
                pe.matmul(bank[4][:, 0:DIM], stT[:, u, :], wmean[:], start=False, stop=True,
                          skip_group_check=True).then_inc(p_ht, 1)

            def x_transpose(u):
                pe.wait_ge(v_xn, u + 1)
                if u >= TILES:
                    pe.wait_ge(v_h, u - 2)
                pe.transpose(bank[4][:, 2 * P:3 * P], xn[:, u % 2, 0:P], ident)
                pe.transpose(bank[4][0:64, 3 * P:4 * P], xn[:, u % 2, P:DIM], ident).then_inc(p_xt, 1)

            def qk_rotary(u):
                w = lws[:, L_QKV1:L_O1].rearrange("p (k n) -> p k n", k=2)
                pe.wait_ge(a_xt, u + 1)
                if u >= 1:
                    pe.wait_ge(a_kt, u)
                pe.matmul(bank[6][:, 0:2 * DIM], xT[:, 0, :], w[:, 0, 0:2 * DIM], start=True, stop=False)
                pe.matmul(bank[6][:, 0:2 * DIM], xT[0:64, 1, :], w[0:64, 1, 0:2 * DIM],
                          start=False, stop=True).then_inc(p_qk, 1)

            def values(u):
                w = lws[:, L_QKV1:L_O1].rearrange("p (k n) -> p k n", k=2)
                if u >= 1:
                    pe.wait_ge(a_v, u)
                pe.matmul(bank[7][:, 0:DIM], xT[:, 0, :], w[:, 0, 2 * DIM:3 * DIM], start=True, stop=False)
                pe.matmul(bank[7][:, 0:DIM], xT[0:64, 1, :], w[0:64, 1, 2 * DIM:3 * DIM],
                          start=False, stop=True).then_inc(p_v, 1)

            def low_rank(u):
                pe.wait_ge(a_xt, u + 1)
                w = lws[:, L_AR:L_P2].rearrange("p (k n) -> p k n", k=2)
                pe.matmul(bank[4][:, 0:P + EXP], xT[:, 0, :], w[:, 0], start=True, stop=False)
                pe.matmul(bank[4][:, 0:P + EXP], xT[0:64, 1, :], w[0:64, 1], start=False, stop=True).then_inc(p_ar, 1)

            def qkv_direct(u):
                w = lws[:, L_QKV2:L_QKV2 + 3 * DIM]
                pe.wait_ge(a_kt, u)
                pe.matmul(bank[6][:, 0:2 * DIM], xT[:, 0, :], w[:, 0:2 * DIM], start=True, stop=False)
                pe.wait_ge(a_v, u)
                pe.matmul(bank[7][:, 0:DIM], xT[:, 0, :], w[:, 2 * DIM:3 * DIM], start=True, stop=False)

            def qkv_experts(u):
                w = lws[:, L_QKV2:L_AR].rearrange("p (k n) -> p k n", k=3)
                pe.wait_ge(a_hw, u - TILES + 1)
                pe.matmul(bank[6][:, 0:2 * DIM], xwT[0:KB, :], w[0:KB, 1, 0:2 * DIM], start=False, stop=False)
                pe.matmul(bank[6][:, 0:2 * DIM], hwT[:], w[:, 2, 0:2 * DIM], start=False, stop=True).then_inc(p_qk, 1)
                pe.matmul(bank[7][:, 0:DIM], xwT[0:KB, :], w[0:KB, 1, 2 * DIM:3 * DIM], start=False, stop=False)
                pe.matmul(bank[7][:, 0:DIM], hwT[:], w[:, 2, 2 * DIM:3 * DIM], start=False, stop=True).then_inc(p_v, 1)

            def hw_transpose(u):
                pe.wait_ge(v_hw, u - TILES + 1)
                pe.wait_ge(a_qt, u)
                pe.transpose(bank[5][:, 0:P], hw[:], ident)
                pe.transpose(bank[5][0:KB, P:2 * P], xn[:, u % 2, P:LIN], ident).then_inc(p_hw, 1)

            def qk_transpose(u):
                if u < TILES:
                    pe.wait_ge(g_qr, u + 1)
                else:
                    pe.wait_ge(a_qr, u - TILES + 1)
                q = qr[:, u % 2].rearrange("p (k b g) d -> p k b (g d)", k=2, b=3)
                for b in range(3):
                    mm = pe.transpose(bank[5][:, b * P:(b + 1) * P], q[:, 0, b, :], ident)
                mm.then_inc(p_qt, 1)
                for b in range(3):
                    mm = pe.transpose(bank[6][:, b * P:(b + 1) * P], q[:, 1, b, :], ident)
                mm.then_inc(p_kt, 1)

            def scores(u):
                pe.wait_ge(a_qt, u + 1)
                pe.wait_ge(a_kt, u + 1)
                if u >= 1:
                    pe.wait_ge(v_p, u)
                masked = u < TILES
                if masked:
                    pe.wait_ge(g_fill, 6)
                    for y in range(2):
                        pe.matmul(bank[y][:, 0:6 * SEQ], identb, maskb, start=True, stop=True,
                                  skip_group_check=True)
                for b in range(3):
                    for i in range(2):
                        for r in range(4):
                            y, s = r // 2, r % 2
                            col = (2 * b + i) * SEQ
                            mm = pe.matmul(bank[y][SLOT * s:SLOT * s + SLOT, col:col + SEQ],
                                           qT[32 * r:32 * r + HD, u % 2, b, SLOT * i:SLOT * i + SLOT],
                                           kT[32 * r:32 * r + HD, u % 2, b, SLOT * i:SLOT * i + SEQ],
                                           start=not masked, stop=True,
                                           tile_position=(32 * r, SLOT * s), skip_group_check=True)
                mm.then_inc(p_s, 1)

            def p_transpose(u):
                pe.wait_ge(a_e, u + 1)
                if u >= 1:
                    pe.wait_ge(v_on, u)
                for g in range(6):
                    mm = pe.transpose(bank[2 + g // 3][:, (g % 3) * P:(g % 3) * P + P],
                                      pr[:, g].rearrange("p i k -> p (i k)"), ident)
                mm.then_inc(p_pt, 1)

            def attend(u, y):
                pe.wait_ge(a_pt, u + 1)
                pe.wait_ge(a_v, u + 1)
                for b in range(3):
                    g = 3 * y + b
                    for i in range(2):
                        for s in range(2):
                            h = 4 * b + 2 * y + s
                            col = g * (HD + 1)
                            mm = pe.matmul(bank[2 + i][SLOT * s:SLOT * s + SLOT, col:col + HD + 1],
                                           pT[SLOT * i:SLOT * i + SEQ, g, s, :],
                                           vs[SLOT * i:SLOT * i + SEQ, u % 2, h, :],
                                           start=True, stop=True, tile_position=(SLOT * i, SLOT * s))
                mm.then_inc(p_o, 1)

            def o_transpose(u):
                pe.wait_ge(v_on, u + 1)
                if u + 2 < UNITS:
                    pe.wait_ge(a_xt, u + 3)
                if TILES <= u + 2 < UNITS:
                    pe.wait_ge(v_lg, u + 3 - TILES)
                if u >= 1:
                    pe.wait_ge(v_h, u)
                for i in range(2):
                    mm = pe.transpose(bank[4][0:96, i * P:(i + 1) * P], on[:, i].rearrange("p g d -> p (g d)"), ident)
                mm.then_inc(p_ot, 1)

            def project(u):
                pe.wait_ge(a_ot, u + 1)
                at = L_O1 if u < TILES else L_P2
                for s in range(2):
                    mm = pe.matmul(bank[4][:, 2 * P:2 * P + DIM], oT[:, s, :], lws[0:96, at + s * DIM:at + (s + 1) * DIM],
                                   start=(s == 0), stop=(s == 1))
                mm.then_inc(p_pr, 1)

            for u in range(UNITS + 2):
                a, b = u - 1, u - 2
                layer1, layer2 = u < TILES, TILES <= u < UNITS
                if layer1:
                    embed_token(u)
                if layer2:
                    x_transpose(u)
                if b >= 0:
                    attend(b, 0)
                if 0 <= a < UNITS:
                    qk_transpose(a)
                if b >= 0:
                    attend(b, 1)
                if layer1:
                    x_transpose(u)
                if layer2:
                    low_rank(u)
                if 0 <= a < UNITS:
                    scores(a)
                if b >= 0:
                    o_transpose(b)
                if layer1:
                    qk_rotary(u)
                if layer2:
                    qkv_direct(u)
                if b >= 0:
                    project(b)
                if layer2:
                    hw_transpose(u)
                if 0 <= a < UNITS:
                    p_transpose(a)
                if layer1:
                    values(u)
                if layer2:
                    qkv_experts(u)


def shape_constants():
    import numpy as np
    c = np.zeros((P, C_N), np.float32)
    tok = np.arange(P) % SLOT
    real = (tok < NPATCH).astype(np.float32)
    c[:, C_ID:C_ID + P] = np.eye(P)
    for g in range(4):
        c[32 * g, C_SELW:C_SELW + P] = 1
        c[32 * g + 1, C_SELB:C_SELB + P] = real
        c[32 * g, C_SELS + g // 2] = 1 / PDIM
    c[0, C_MEAN] = c[32, C_MEAN] = -1 / PDIM
    c[:, C_STACK:C_STACK + 64] = np.tile(np.eye(64), (2, 1))
    pos = np.where(tok < NPATCH, tok + 1, 0).astype(np.float32)
    freq = np.float32(10000.0) ** (-np.arange(0, HD, 2, dtype=np.float32) / HD)
    ang = (pos[:, None] * freq[None, :]).astype(np.float32)
    c[:, C_COS:C_COS + HD] = np.tile(np.cos(ang), (1, 2))
    c[:, C_SIN:C_SIN + HD] = np.tile(np.sin(ang), (1, 2))
    c[:, C_TOK], c[:, C_NTOK], c[:, C_ONE] = real, 1 - real, 1
    right = np.arange(P) >= 64
    c[:, C_W0], c[:, C_W1] = 1 + right, 2 - right
    c[:, C_IOTA:C_IOTA + EXP] = np.arange(EXP)
    c[:, C_HALF:C_HALF + TILES] = -0.5
    place = np.r_[np.arange(1, SEQ), 0]
    hidden = np.where(place[None, :] > place[:, None], np.float32(-1e30), np.float32(0))
    for s in range(2):
        c[SLOT * s:SLOT * s + SEQ, C_MASK:C_N] = np.tile(hidden, (1, 6))
    return c


def kernel(**inputs):
    import numpy as np
    import concourse.bacc as bacc
    from concourse.bass_utils import run_bass_kernel_spmd

    a = {k: np.asarray(v) for k, v in inputs.items()}
    x = a["x"].reshape(IMG, CH, ROWS, 8, GRID, 2, 8)
    xp = np.zeros((2, 8, 8, CH, IMG, ROWS, WINS), np.float32)
    xp[1, :, :, :, :, :, 0:GRID] = x[:, :, :, :, :, 0].transpose(3, 5, 1, 0, 2, 4)
    xp[0, :, :, :, :, :, 1:WINS] = x[:, :, :, :, :, 1].transpose(3, 5, 1, 0, 2, 4)
    xp = xp.reshape(P, CH, IMG * ROWS * WINS)

    def tok_tiles(w):
        w = w.reshape(-1, 2, 8, 16, 5, CH)
        t = np.zeros((2, 8, 8, CH, 10, w.shape[0]), np.float32)
        copy = {(0, 0): 1, (1, 1): 2, (0, 1): 3, (1, 0): 4}
        for k in range(8):
            kind, a2, half = k // 4, (k // 2) % 2, k % 2
            row = 1 + a2 if kind == 0 else 3 * a2
            s = w[:, row % 2, :, :, copy[(row // 2, half)], :].reshape(-1, 8, 2, 8, CH)
            t[:, :, :, :, k] = s.transpose(2, 1, 3, 4, 0)
        for a2 in range(2):
            s = w[:, a2, :, :, 0, :].reshape(-1, 8, 2, 8, CH).transpose(2, 1, 3, 4, 0)
            t[1, :, :, :, 8 + a2], t[0, :, :, :, 8 + a2] = s[0], s[1]
        return t.reshape(P, CH, 10, -1)

    tokw = tok_tiles(a["L0_tok_W"])
    tokgb = tok_tiles(np.stack([a["L0_tok_ln_gamma"], a["L0_tok_ln_beta"]])).reshape(P, CH * 10, 2)
    cls = np.zeros((P, 2), np.float32)
    cls[:, 0] = a["cls_tok"].reshape(DIM)[:P]
    cls[:DIM - P, 1] = a["cls_tok"].reshape(DIM)[P:]

    lnb = np.zeros((1, DIM + P), np.float32)
    lnb[0, :DIM] = a["L0_tok_b"]
    lnb[0, DIM:] = np.arange(P) % SLOT < NPATCH

    lw = np.zeros((P, L_N), np.float32)

    def put(at, w):
        n = w.shape[1]
        lw[:, at:at + n] = w[:P]
        lw[:w.shape[0] - P, at + n:at + 2 * n] = w[P:]

    halves = np.r_[np.arange(0, HD, 2), np.arange(1, HD, 2)]
    wq, wk = (a[f"L0_attn_{n}"].reshape(HEADS, HD, DIM)[:, halves].reshape(DIM, DIM) for n in ("wq", "wk"))
    put(L_QKV1, np.concatenate([wq, wk, a["L0_attn_wv"]]).T)
    wqkv = np.concatenate([a["L0_ffn_Wqkv"].T, a["L0_ffn_bb"], a["L0_ffn_bqkv"][None]])
    put(L_QKV2, wqkv)
    lw[:, L_QKV2 + 6 * DIM:L_AR] = a["L0_ffn_Bm"].transpose(0, 2, 1).reshape(EXP * RANK, 3 * DIM)
    put(L_AR, np.concatenate([a["L0_ffn_A"].reshape(EXP * RANK, DIM), a["L0_ffn_Wg"]]).T)
    for at, w in ((L_O1, a["L0_attn_wo"]), (L_P2, a["L0_ffn_Wproj"])):
        w = w.T.reshape(3, 2, 2, HD, DIM).transpose(1, 0, 3, 2, 4).reshape(96, 2 * DIM)
        lw[:96, at:at + 2 * DIM] = w
    lw[:, L_BAR:L_BAR + P] = a["L0_ffn_ba"].reshape(1, -1)
    lw[:, L_BAR + P:L_BP] = a["L0_ffn_bg"][None]
    lw[:, L_BP:L_N] = a["L0_ffn_bproj"][None]

    arrays = {"in_x": xp, "in_tokw": tokw, "in_tokgb": tokgb, "in_b": lnb, "in_cls": cls,
              "in_lw": lw, "in_con": shape_constants()}
    arrays = {k: np.ascontiguousarray(v) for k, v in arrays.items()}
    nc = bacc.Bacc("TRN2", target_bir_lowering=False, num_devices=1)
    args = [nc.dram_tensor(k, v.shape, mybir.dt.from_np(v.dtype), kind="ExternalInput").ap() for k, v in arrays.items()]
    out = nc.dram_tensor("out", (TILES, P, DIM), F32, kind="ExternalOutput").ap()
    vit_tower(nc, *args, out)
    got = run_bass_kernel_spmd(nc, [arrays], core_ids=[0]).results[0]["out"]
    got = got.reshape(IMG, SLOT, DIM)
    return np.concatenate([got[:, NPATCH:SEQ], got[:, 0:NPATCH]], axis=1)
```

```python
from contextlib import ExitStack

import concourse.bass as bass
from concourse import mybir
from concourse.alu_op_type import AluOpType as ALU

F32 = mybir.dt.float32
F32R = mybir.dt.float32r
BF16 = mybir.dt.bfloat16
U32 = mybir.dt.uint32
ACT = mybir.ActivationFunctionType
AX_X = mybir.AxisListType.X

P = 128
IMG = 16
CH = 3
GRID = 6
ROWS = 2 * GRID
WINS = GRID + 1
NPATCH = GRID * GRID
SEQ = NPATCH + 1
DIM = 192
HEADS = 12
HD = DIM // HEADS
EXP = 8
RANK = 16
TILES = IMG // 2
SLOT = 64
PDIM = 16 * 16 * 5 * CH
LN_EPS = 1e-5
LIN = DIM + EXP + 1
KB = DIM - P + EXP + 1
HCELLS = IMG // 2 * ROWS * WINS
HALF = IMG // 2 * NPATCH
SMAX_SCALE = HD ** -0.5

C_ID = 0
C_SELW = C_ID + P
C_SELB = C_SELW + P
C_STACK = C_SELB + P
C_COS = C_STACK + 64
C_SIN = C_COS + HD
C_TOK = C_SIN + HD
C_NTOK = C_TOK + 1
C_ONE = C_NTOK + 1
C_W0 = C_ONE + 1
C_W1 = C_W0 + 1
C_SELS = C_W1 + 1
C_IOTA = C_SELS + 2
C_HALF = C_IOTA + EXP
C_MEAN = C_HALF + TILES
C_MASK = C_MEAN + 1
C_N = C_MASK + 4 * SEQ

L_QKV1 = 0
L_O1 = L_QKV1 + 2 * 3 * DIM
L_QKV2 = L_O1 + 2 * DIM
L_AR = L_QKV2 + 3 * 3 * DIM
L_P2 = L_AR + 2 * (P + EXP)
L_BAR = L_P2 + 2 * DIM
L_BP = L_BAR + P + EXP
L_N = L_BP + DIM


def vit_tower(nc, x, tokw, tokgb, lnb, cls, lw, con, out):
    with ExitStack() as ctx:
        def sb(name, shape, dt=F32):
            return ctx.enter_context(nc.sbuf_tensor(name, shape, dt))

        def sem(name):
            return ctx.enter_context(nc.semaphore(name))

        xin = sb("xin", [P, CH, IMG * ROWS * WINS])
        xh = sb("xh", [P, CH, IMG * ROWS * WINS], F32R)
        xl = sb("xl", [P, CH, IMG * ROWS * WINS], F32R)
        xsum = sb("xsum", [P, IMG * ROWS * WINS])
        xsq = sb("xsq", [P, 2, IMG * ROWS * WINS])
        win = sb("win", [P, CH, 10, DIM])
        wg = sb("wg", [P, 2, 10, DIM])
        ws = sb("ws", [P, CH, 8, 3 * P], F32R)
        gb = sb("gb", [P, CH * 10, 2])
        brow = sb("brow", [1, DIM + P])
        clsT = sb("clsT", [P, 2])
        cn = sb("cn", [P, C_N])
        idle = sb("idle", [P, 512], BF16)
        mk = sb("mk", [P, P + 4 * SEQ], BF16)
        lws = sb("lws", [P, L_N])
        eT = sb("eT", [P, 2, TILES, P])
        rows = sb("rows", [P, DIM])
        wmean = sb("wmean", [P, DIM])
        stT = sb("stT", [P, TILES, P])
        bmrep = sb("bmrep", [P, DIM])
        st = sb("st", [P, 8, TILES])
        hid = sb("hid", [P, TILES, DIM])
        bns = sb("bns", [P, 2, 6])
        mv = sb("mv", [P, 2, 4])
        xn = sb("xn", [P, 2, LIN + 7])
        xd = sb("xd", [P, 2, 2, DIM - P])
        xT = sb("xT", [P, 2, P])
        xTh = sb("xTh", [P, 2 * P], F32R)
        xTl = sb("xTl", [P, P], F32R)
        wTh, wTl = (v[:, 0, 0:6 * DIM].rearrange("p (k n) -> p k n", k=2) for v in (xh, xl))
        w2h, w2l = (v[:, 1:3].rearrange("p c n -> p (c n)")[:, 0:9 * DIM].rearrange("p (k n) -> p k n", k=3)
                    for v in (xh, xl))
        hwTh = sb("hwTh", [P, 2 * P], F32R)
        hwTl = sb("hwTl", [P, 2 * P], F32R)
        hal = sb("hal", [P, P + EXP])
        rt = sb("rt", [P, 8, EXP])
        rti = sb("rti", [P, EXP], U32)
        hw = sb("hw", [P, P])
        rc = win[:, 0, 0:2].rearrange("p a (g d) -> p (a g) d", d=HD)
        rs = win[:, 0, 2:4].rearrange("p a (g d) -> p (a g) d", d=HD)
        qr = sb("qr", [P, 2, 3 * DIM + 2 * HD])
        vs = sb("vs", [P, 3, HEADS, 32])
        qT = win[:, 1].rearrange("p k n -> p (k n)")[0:96, 0:4 * P].rearrange("p (u b t) -> p u b t", u=2, b=2)
        kT = win[:, 2].rearrange("p k n -> p (k n)")[0:96, 0:8 * P].rearrange("p (u b t) -> p u b t", u=2, b=4)
        pr = sb("pr", [P, 2, 6, 2, SLOT])
        mx = sb("mx", [P, HEADS])
        pT = sb("pT", [P, 6, 2, SLOT])
        rec = sb("rec", [P, 2, HEADS])
        oT = sb("oT", [P, 2, P])

        pso = ctx.enter_context(nc.psum_tensor("pso", [P, 3, 512], F32))
        ppt = ctx.enter_context(nc.psum_tensor("ppt", [P, 2, 512], F32))
        bank = [pso[:, 0, :], pso[:, 1, :], ppt[:, 0, :], ppt[:, 1, :]]
        bank += [ctx.enter_context(nc.psum_tensor(f"bank{i}", [P, 512], F32)) for i in range(4, 7)]
        bank += [pso[:, 2, :]]

        ident = cn[:, C_ID:C_ID + P]
        identb = mk[:, 0:P]
        maskb = mk[:, P:P + 4 * SEQ]

        d_x = [[sem(f"d_x{c}_first"), sem(f"d_x{c}_rest")] for c in range(CH)]
        d_w = [[sem(f"d_w{c}_outer"), sem(f"d_w{c}_centre")] for c in range(CH)]
        d_gb, d_cn, d_misc, d_lw, d_out = sem("d_gb"), sem("d_cn"), sem("d_misc"), sem("d_lw"), sem("d_out")
        zeros_for_warmup = sem("zeros_for_warmup")
        dve_filled = sem("dve_filled")
        weights_scaled = sem("weights_scaled")
        pixels_low = sem("pixels_low")
        weights_low = sem("weights_low")
        weight_sums_out = sem("weight_sums_out")
        variances_ready = sem("variances_ready")
        embed_low_out = sem("embed_low_out")
        dve_done = sem("dve_done")
        token_variance = sem("token_variance")
        tokens_normed = sem("tokens_normed")
        tokens_low = sem("tokens_low")
        tokens_low2 = sem("tokens_low2")
        w1_low = sem("w1_low")
        rope_products = sem("rope_products")
        keys_rotated = sem("keys_rotated")
        scores_shifted = sem("scores_shifted")
        probs_ready = sem("probs_ready")
        residual_added = sem("residual_added")
        logits_shifted = sem("logits_shifted")
        states_scaled = sem("states_scaled")
        states_low = sem("states_low")
        last_scores_shifted = sem("last_scores_shifted")
        last_probs_ready = sem("last_probs_ready")
        pixels_high = sem("pixels_high")
        weights_high = sem("weights_high")
        pixels_squared = sem("pixels_squared")
        w1_high = sem("w1_high")
        w2_high = sem("w2_high")
        embed_high_out = sem("embed_high_out")
        patch_sums_out = sem("patch_sums_out")
        tokens_t_out = sem("tokens_t_out")
        tokens_high2 = sem("tokens_high2")
        values_out = sem("values_out")
        queries_t_out = sem("queries_t_out")
        keys_t_out = sem("keys_t_out")
        qk_slots2 = sem("qk_slots2")
        exps_ready = sem("exps_ready")
        probs_t_out = sem("probs_t_out")
        attended_out = sem("attended_out")
        router_exps = sem("router_exps")
        states_high = sem("states_high")
        last_exps_ready = sem("last_exps_ready")
        last_probs_t_out = sem("last_probs_t_out")
        pool_filled = sem("pool_filled")
        channel_sums = sem("channel_sums")
        patch_rstd = sem("patch_rstd")
        token_rstd = sem("token_rstd")
        queries_rotated = sem("queries_rotated")
        w2_low = sem("w2_low")
        bias_added = sem("bias_added")
        embed_summed = sem("embed_summed")
        weight_sums = sem("weight_sums")
        patch_sums = sem("patch_sums")
        patch_means = sem("patch_means")
        weight_sums_spread = sem("weight_sums_spread")
        embed_tokens = sem("embed_tokens")
        tokens_t = sem("tokens_t")
        qk_ready = sem("qk_ready")
        values_ready = sem("values_ready")
        queries_t = sem("queries_t")
        keys_t = sem("keys_t")
        scores_ready = sem("scores_ready")
        probs_t = sem("probs_t")
        last_probs_t = sem("last_probs_t")
        attended = sem("attended")
        projected = sem("projected")
        low_rank_ready = sem("low_rank_ready")
        states_t = sem("states_t")

        block = ctx.enter_context(nc.Block())

        UNITS = 2 * TILES

        w_qkv2 = lws[:, L_QKV2:L_AR].rearrange("p (k n) -> p k n", k=3)
        w_qkv1 = lws[:, L_QKV1:L_O1].rearrange("p (k n) -> p k n", k=2)

        def q_slots(u):
            return qr[:, u % 2, 0:DIM].rearrange("p (h d) -> p h d", d=HD)

        def k_slots(u):
            k = qr[:, u % 2, DIM:DIM + 2 * (DIM + HD)].rearrange("p (e c) -> p e c", e=2)
            return k[:, :, 0:DIM].rearrange("p e (n c) -> p e n c", c=32)[:, :, :, 0:HD]

        def by_parity(k):
            return k.rearrange("p (n e) d -> p e n d", e=2)

        def cells_of(h):
            return slice(h * HCELLS, (h + 1) * HCELLS)

        LAST = UNITS - 1
        last_pt_banks = [bank[5], bank[0], bank[1]]

        def last_probs(r):
            return pr[:, LAST % 2, 2 * r:2 * r + 2, :, 0:SEQ].rearrange("p e i k -> p (e i) k")

        def x_bank(u):
            return bank[7 if u <= TILES else 4]

        @block.sync
        def _(sp):
            sp.dma_start(gb[:], tokgb).then_inc(d_gb, 16)
            for c in range(CH):
                for h in range(2):
                    sp.dma_start(xin[:, c, cells_of(h)], x[:, c, cells_of(h)]).then_inc(d_x[c][h], 16)
                if c:
                    sp.dma_start(win[:, c, 0:4], tokw[:, c, 0:4]).then_inc(d_w[c][0], 16)
                sp.dma_start(win[:, c, 4:10], tokw[:, c, 4:10]).then_inc(d_w[c][1], 16)
                if c == 1:
                    sp.dma_start(cn[:], con).then_inc(d_cn, 16)
            sp.dma_start(brow[:], lnb).then_inc(d_misc, 16)
            sp.dma_start(clsT[:], cls).then_inc(d_misc, 16)
            sp.dma_start(lws[:], lw).then_inc(d_lw, 16)
            for t in range(TILES):
                sp.wait_ge(residual_added, TILES + t + 1)
                sp.dma_start(out[t], hid[:, t, :]).then_inc(d_out, 16)
            sp.wait_ge(d_out, 16 * TILES)

        @block.gpsimd
        def _(pool):
            nc.gpsimd.memset(qr[:], 0.0).then_inc(pool_filled, 1)
            nc.gpsimd.memset(pr[:], 0.0).then_inc(pool_filled, 1)
            nc.gpsimd.memset(pT[:], 0.0).then_inc(pool_filled, 1)
            nc.gpsimd.memset(vs[:], 0.0).then_inc(pool_filled, 1)
            nc.gpsimd.memset(xn[:], 1.0).then_inc(pool_filled, 1)
            pool.wait_ge(d_cn, 16)
            nc.gpsimd.tensor_copy(mk[:, 0:P], cn[:, C_ID:C_ID + P])
            nc.gpsimd.tensor_copy(mk[:, P:P + 4 * SEQ], cn[:, C_MASK:C_N]).then_inc(pool_filled, 1)
            for c in range(2):
                for h in range(2):
                    pool.wait_ge(d_x[c][h], 16)
            nc.gpsimd.tensor_tensor(xsum[:], xin[:, 0], xin[:, 1], ALU.add).then_inc(channel_sums, 1)
            pool.wait_ge(pixels_squared, 2)
            nc.gpsimd.tensor_tensor(xsq[:, 1], xsq[:, 0], xsq[:, 1], ALU.add).then_inc(channel_sums, 1)
            for h in range(2):
                pool.wait_ge(d_x[2][h], 16)
            pool.wait_ge(channel_sums, 1)
            nc.gpsimd.tensor_tensor(xsum[:], xsum[:], xin[:, 2], ALU.add).then_inc(channel_sums, 1)
            pool.wait_ge(pixels_squared, 3)
            pool.wait_ge(channel_sums, 2)
            nc.gpsimd.tensor_tensor(xsq[:, 1], xsq[:, 1], xsq[:, 0], ALU.add).then_inc(channel_sums, 1)
            pool.wait_ge(variances_ready, 1)
            nc.gpsimd.tensor_tensor(st[:, 3, :], st[:, 2, :], cn[:, C_HALF:C_HALF + TILES], ALU.pow).then_inc(patch_rstd, 1)

            def root(u):
                pool.wait_ge(token_variance, u + 1)
                if u >= 2:
                    pool.wait_ge(tokens_normed, u - 1)
                nc.gpsimd.tensor_tensor(mv[:, u % 2, 3:4], mv[:, u % 2, 2:3], cn[:, C_HALF:C_HALF + 1],
                                        ALU.pow).then_inc(token_rstd, 1)

            def rotate(u):
                h = HD // 2
                if u >= 2:
                    pool.wait_ge(keys_t, u - 1)
                pool.wait_ge(rope_products, 2 * u + 1)
                for lo, hi, op in ((0, h, ALU.subtract), (h, HD, ALU.add)):
                    nc.gpsimd.tensor_tensor(q_slots(u)[:, :, lo:hi], rc[:, 0:HEADS, lo:hi],
                                            rs[:, 0:HEADS, h - lo:2 * h - lo], op)
                pool.wait_ge(rope_products, 2 * u + 2)
                nc.gpsimd.tensor_tensor(k_slots(u)[:, :, :, 0:h], by_parity(rc[:, HEADS:2 * HEADS, 0:h]),
                                        by_parity(rs[:, HEADS:2 * HEADS, h:HD]), ALU.subtract).then_inc(queries_rotated, 1)

            def add_bias(u):
                pool.wait_ge(tokens_normed, u + 1)
                pool.wait_ge(d_lw, 16)
                nc.gpsimd.tensor_tensor(hid[:, u % TILES, :], hid[:, u % TILES, :], lws[:, L_BP:L_BP + DIM],
                                        ALU.add).then_inc(bias_added, 1)

            def w2_rest(k):
                pool.wait_ge(w2_high, k + 1)
                nc.gpsimd.tensor_tensor(w2l[:, k], w_qkv2[:, k], w2h[:, k].bitcast(F32), ALU.subtract).then_inc(w2_low, 1)

            root(0)
            for u in range(UNITS):
                if u + 1 < UNITS:
                    root(u + 1)
                if u < TILES:
                    rotate(u)
                if 2 <= u < 5:
                    w2_rest(u - 2)
                if TILES <= u + 1 < UNITS:
                    add_bias(u + 1)

        @block.scalar
        def _(act):
            act.dma_start(win[:, 0, 0:4], tokw[:, 0, 0:4]).then_inc(d_w[0][0], 16)

            def x_high(c):
                for h in range(2):
                    cells = cells_of(h)
                    act.wait_ge(d_x[c][h], 16)
                    nc.scalar.activation(xh[:, c, cells], xin[:, c, cells], ACT.Copy).then_inc(pixels_high, 1)

            def w_high(c, part):
                k = slice(4 * part, 4 * part + 4)
                act.wait_ge(weights_scaled, 2 * c + part + 1)
                nc.scalar.activation(ws[:, c, k, 0:P], wg[:, c % 2, k, 0:P], ACT.Copy)
                nc.scalar.activation(ws[:, c, k, 2 * P:2 * P + 64], wg[:, c % 2, k, P:DIM],
                                     ACT.Copy).then_inc(weights_high, 1)

            def square(c):
                if c == 2:
                    act.wait_ge(channel_sums, 2)
                nc.scalar.activation(xsq[:, c % 2], xin[:, c], ACT.Square).then_inc(pixels_squared, 1)

            w_high(0, 0)
            x_high(0)
            for c in range(CH):
                if c:
                    w_high(c, 0)
                square(c)
                if c + 1 < CH:
                    x_high(c + 1)
                w_high(c, 1)
            act.wait_ge(d_lw, 16)
            act.wait_ge(weight_sums, 1)
            nc.scalar.activation(wTh, w_qkv1, ACT.Copy).then_inc(w1_high, 1)
            act.wait_ge(dve_filled, 3)
            act.wait_ge(patch_sums, 1)
            for i in range(2):
                nc.scalar.activation(
                    stT[:, 4 * i:4 * i + 4, :].rearrange("p t (s q) -> p t s q", s=2)[:, :, :, 0:NPATCH],
                    bank[5 + i][:, 0:HALF].rearrange("p (t s q) -> p t s q", t=4, s=2), ACT.Copy).then_inc(patch_sums_out, 1)

            def embed_evac(i):
                act.wait_ge(embed_summed, i + 1)
                nc.scalar.activation(
                    eT[:, 0, 4 * i:4 * i + 4, :].rearrange("p t (s q) -> p t s q", s=2)[:, :, :, 0:NPATCH],
                    bank[2 * i][:, 0:HALF].rearrange("p (t s q) -> p t s q", t=4, s=2), ACT.Copy).then_inc(embed_high_out, 1)

            def xt_evac(u):
                act.wait_ge(tokens_t, u + 1)
                if u >= 1:
                    act.wait_ge(values_ready, u)
                b = x_bank(u)
                if u < TILES:
                    nc.scalar.activation(xTh[:], b[:, 0:2 * P], ACT.Copy).then_inc(tokens_t_out, 1)
                    return
                nc.scalar.activation(xT[0:64, 1, :], b[0:64, P:2 * P], ACT.Copy)
                nc.scalar.activation(xT[:, 0, :], b[:, 0:P], ACT.Copy).then_inc(tokens_t_out, 1)

            def router_exp(u):
                act.wait_ge(logits_shifted, u - TILES + 1)
                nc.scalar.activation(rt[:, 2, :], rt[:, 1, :], ACT.Exp, accum_out=rt[:, 3, 0:1]).then_inc(router_exps, 1)

            def hw_evac(u):
                act.wait_ge(states_t, u - TILES + 1)
                nc.scalar.activation(hwTh[0:KB, P:2 * P], bank[5][0:KB, P:2 * P], ACT.Copy)
                nc.scalar.activation(hwTh[:, 0:P], bank[5][:, 0:P], ACT.Copy).then_inc(states_high, 1)

            def qr_evac(u):
                act.wait_ge(qk_ready, u + 1)
                act.wait_ge(keys_t, u - 1)
                nc.scalar.activation(q_slots(u), bank[6][:, 0:DIM].rearrange("p (h d) -> p h d", d=HD), ACT.Copy)
                nc.scalar.activation(k_slots(u), by_parity(bank[6][:, DIM:2 * DIM].rearrange("p (h d) -> p h d", d=HD)),
                                     ACT.Copy).then_inc(qk_slots2, 1)

            def v_evac(u):
                act.wait_ge(pool_filled, 4)
                act.wait_ge(values_ready, u + 1)
                if u >= 3:
                    act.wait_ge(attended, u - 2)
                for s in range(2):
                    h = slice(6 * s, 6 * s + 6)
                    e = nc.scalar.activation(vs[:, u % 3, h, s * HD:s * HD + HD],
                                             bank[7][:, 0:DIM].rearrange("p (h d) -> p h d", d=HD)[:, h], ACT.Copy)
                e.then_inc(values_out, 1)

            def qkt_evac(u):
                act.wait_ge(queries_t, u + 1)
                if u >= 2:
                    act.wait_ge(scores_ready, u - 1)
                nc.scalar.activation(qT[:, u % 2].rearrange("p b t -> p (b t)"), bank[5][0:96, 0:2 * P],
                                     ACT.Copy).then_inc(queries_t_out, 1)
                act.wait_ge(keys_t, u + 1)
                nc.scalar.activation(kT[:, u % 2].rearrange("p b (i k) -> p (b i) k", i=2)[:, :, 0:SEQ],
                                     bank[6][0:96, 0:4 * P].rearrange("p (g k) -> p g k", k=SLOT)[:, :, 0:SEQ],
                                     ACT.Copy).then_inc(keys_t_out, 1)

            def exps(u):
                act.wait_ge(scores_shifted, u + 1)
                p = pr[:, u % 2, :, :, 0:SEQ]
                nc.scalar.activation(p, p, ACT.Exp, scale=SMAX_SCALE).then_inc(exps_ready, 1)

            def pt_evac(u):
                act.wait_ge(pool_filled, 3)
                act.wait_ge(probs_t, u + 1)
                if u >= 1:
                    act.wait_ge(attended, u)
                nc.scalar.activation(pT[:].rearrange("p (y b) s q -> p y (b s) q", y=2)[:, :, :, 0:SEQ],
                                     ppt[:, :, 0:3 * P].rearrange("p y (g q) -> p y g q", q=SLOT)[:, :, :, 0:SEQ],
                                     ACT.Copy).then_inc(probs_t_out, 1)

            def o_evac(u):
                act.wait_ge(attended, u + 1)
                if u >= 1:
                    act.wait_ge(projected, u)
                for k, n in ((0, P), (1, 64)):
                    e = nc.scalar.activation(oT[0:n, k, :].rearrange("p (i q) -> p i q", i=2),
                                             ppt[0:n, :, SLOT * k:SLOT * k + SLOT], ACT.Copy)
                e.then_inc(attended_out, 1)

            def last_exps():
                for r in range(3):
                    act.wait_ge(last_scores_shifted, r + 1)
                    nc.scalar.activation(last_probs(r), last_probs(r), ACT.Exp,
                                         scale=SMAX_SCALE).then_inc(last_exps_ready, 1)

            def last_pt_evac():
                act.wait_ge(attended, LAST)
                for r in range(3):
                    act.wait_ge(last_probs_t, r + 1)
                    nc.scalar.activation(pT[:, 2 * r:2 * r + 2, :, 0:SEQ].rearrange("p b s q -> p (b s) q"),
                                         last_pt_banks[r][:, 0:2 * P].rearrange("p (g q) -> p g q", q=SLOT)[:, :, 0:SEQ],
                                         ACT.Copy).then_inc(last_probs_t_out, 1)

            embed_evac(0)
            xt_evac(0)
            for u in range(UNITS + 2):
                a, b = u - 1, u - 2
                layer1, layer2 = u < TILES, TILES <= u < UNITS
                if 0 < u < UNITS:
                    xt_evac(u)
                if 0 <= a < UNITS:
                    qkt_evac(a)
                if layer2:
                    act.wait_ge(tokens_t_out, u + 1)
                    nc.scalar.activation(xTh[:, 0:P], xT[:, 0, :], ACT.Copy).then_inc(tokens_high2, 1)
                if layer1:
                    if b >= 0:
                        pt_evac(b)
                    if a >= 0:
                        exps(a)
                    v_evac(u)
                    if u == 1:
                        embed_evac(1)
                    if 2 <= u < 5:
                        act.wait_ge(embed_summed, 2)
                        nc.scalar.activation(w2h[:, u - 2], w_qkv2[:, u - 2], ACT.Copy).then_inc(w2_high, 1)
                    if b >= 0:
                        o_evac(b)
                    continue
                if b < LAST:
                    pt_evac(b)
                else:
                    last_pt_evac()
                if layer2:
                    router_exp(u)
                    o_evac(b)
                    hw_evac(u)
                if a < LAST:
                    exps(a)
                elif a == LAST:
                    last_exps()
                if layer2:
                    qr_evac(u)
                    v_evac(u)
                else:
                    o_evac(b)

        @block.vector
        def _(dve):
            made = [0]

            def mark(ins):
                ins.then_inc(dve_done, 1)
                made[0] += 1
                return made[0]

            def after(n):
                dve.wait_ge(dve_done, n)

            nc.vector.memset(idle[:], 0.0).then_inc(zeros_for_warmup, 1)
            nc.vector.memset(bank[4][:, 0:DIM], 0.0).then_inc(dve_filled, 1)
            nc.vector.memset(bank[5][:, 0:HALF], 0.0)
            nc.vector.memset(bank[6][:, 0:HALF], 0.0).then_inc(dve_filled, 1)
            nc.vector.memset(stT[:], 0.0)
            nc.vector.memset(eT[:, 1], 0.0)
            dve.wait_ge(d_gb, 16)

            def w_scale(c, part):
                k = slice(0, 4) if part == 0 else slice(4, 10)
                n = k.stop - k.start
                dve.wait_ge(d_w[c][part], 16)
                if c >= 2:
                    dve.wait_ge(weights_high, 2 * (c - 2) + part + 1)
                g = gb[:, 10 * c + k.start:10 * c + k.stop, 0:1].to_broadcast([P, n, DIM])
                m = nc.vector.tensor_tensor(wg[:, c % 2, k], win[:, c, k], g, ALU.mult)
                if part == 1:
                    after(mark(m))
                    for half in range(2):
                        lo, hi = (64, 128) if half == 0 else (0, 64)
                        ctr = wg[lo:hi, c % 2, 4 + half:8:2, :]
                        m = nc.vector.tensor_tensor(ctr, ctr, wg[lo:hi, c % 2, 8:10, :], ALU.add)
                m.then_inc(weights_scaled, 1)

            def w_low(c, part):
                k = slice(4 * part, 4 * part + 4)
                dve.wait_ge(weights_high, 2 * c + part + 1)
                nc.vector.tensor_tensor(ws[:, c, k, P:2 * P], wg[:, c % 2, k, 0:P], ws[:, c, k, 0:P].bitcast(F32),
                                        ALU.subtract)
                nc.vector.tensor_tensor(ws[:, c, k, 2 * P + 64:3 * P], wg[:, c % 2, k, P:DIM],
                                        ws[:, c, k, 2 * P:2 * P + 64].bitcast(F32), ALU.subtract).then_inc(weights_low, 1)

            def x_low(c):
                for h in range(2):
                    cells = cells_of(h)
                    dve.wait_ge(pixels_high, 2 * c + h + 1)
                    nc.vector.tensor_tensor(xl[:, c, cells], xin[:, c, cells], xh[:, c, cells].bitcast(F32),
                                            ALU.subtract).then_inc(pixels_low, 1)

            w_scale(0, 0)
            for c in range(CH):
                w_low(c, 0)
                x_low(c)
                w_scale(c, 1)
                if c + 1 < CH:
                    w_scale(c + 1, 0)
                w_low(c, 1)
            nc.vector.memset(eT[:, 0], 0.0).then_inc(dve_filled, 1)
            dve.wait_ge(d_lw, 16)
            dve.wait_ge(w1_high, 1)
            nc.vector.tensor_tensor(wTl, w_qkv1, wTh.bitcast(F32), ALU.subtract).then_inc(w1_low, 1)
            dve.wait_ge(d_misc, 32)
            dve.wait_ge(dve_filled, 3)
            cl = eT[:].rearrange("p c t (s q) -> p c t s q", s=2)
            for k in range(2):
                nc.vector.tensor_copy(cl[:, k, :, :, NPATCH],
                                      clsT[:, k:k + 1].unsqueeze(2).to_broadcast([P, TILES, 2]))
            dve.wait_ge(weight_sums, 1)
            nc.vector.tensor_copy(rows[:], bank[4][:, 0:DIM]).then_inc(weight_sums_out, 1)
            dve.wait_ge(d_cn, 16)
            dve.wait_ge(weight_sums_spread, 1)
            nc.vector.tensor_scalar(wmean[:], bank[4][:, 0:DIM], cn[:, C_MEAN:C_MEAN + 1], None, ALU.mult)
            m_rep = mark(nc.vector.tensor_copy(bmrep[:], bank[4][:, DIM:2 * DIM]))
            dve.wait_ge(patch_means, 1)
            sp_ = bank[6][:, 0:2 * TILES].rearrange("p (t k) -> p k t", k=2)
            m = mark(nc.vector.tensor_copy(st[:, 0:2, :], sp_))
            after(m)
            m = mark(nc.vector.tensor_tensor(st[:, 4, :], st[:, 0, :], st[:, 0, :], ALU.mult))
            after(m)
            m = mark(nc.vector.tensor_tensor(st[:, 5, :], st[:, 1, :], st[:, 4, :], ALU.subtract))
            after(m)
            nc.vector.tensor_scalar(st[:, 2, :], st[:, 5, :], 0.0, LN_EPS, ALU.max, ALU.add).then_inc(variances_ready, 1)

            def embed_low(i):
                dve.wait_ge(embed_summed, i + 1)
                nc.vector.tensor_copy(cl[:, 1, 4 * i:4 * i + 4, :, 0:NPATCH],
                                      bank[2 * i + 1][:, 0:HALF].rearrange("p (t s q) -> p t s q", t=4, s=2)
                                      ).then_inc(embed_low_out, 1)

            embed_low(0)
            dve.wait_ge(patch_rstd, 1)
            m = mark(nc.vector.tensor_scalar(st[:, 6, :], st[:, 3, :], cn[:, C_TOK:C_TOK + 1],
                                             cn[:, C_NTOK:C_NTOK + 1], ALU.mult, ALU.add))
            after(m)
            after(m_rep)

            def token(u):
                dve.wait_ge(embed_tokens, u + 1)
                m = mark(nc.vector.scalar_tensor_tensor(hid[:, u, :], bank[5][:, 0:DIM], st[:, 6, u:u + 1],
                                                        bmrep[:], ALU.mult, ALU.add))
                after(m)

            def stats(u):
                if u >= TILES:
                    dve.wait_ge(residual_added, u - TILES + 1)
                m = mark(nc.vector.bn_stats(bns[:, u % 2, :], hid[:, u % TILES, :]))
                after(m)
                m = mark(nc.vector.bn_aggr(mv[:, u % 2, 0:2], bns[:, u % 2, :]))
                after(m)
                nc.vector.tensor_scalar(mv[:, u % 2, 2:3], mv[:, u % 2, 1:2], LN_EPS, None,
                                        ALU.add).then_inc(token_variance, 1)

            def normalise(u):
                if u == 0:
                    dve.wait_ge(pool_filled, 5)
                dve.wait_ge(token_rstd, u + 1)
                if u >= 2:
                    dve.wait_ge(tokens_t, u - 1)
                if u >= TILES + 2:
                    dve.wait_ge(states_t, u - TILES - 1)
                n = P if u < TILES else DIM
                last = nc.vector.tensor_scalar(xn[:, u % 2, 0:n], hid[:, u % TILES, 0:n], mv[:, u % 2, 0:1],
                                               mv[:, u % 2, 3:4], ALU.subtract, ALU.mult)
                if u < TILES:
                    twice = hid[:, u, P:DIM].unsqueeze(1).to_broadcast([P, 2, DIM - P])
                    last = nc.vector.tensor_scalar(xd[:, u % 2], twice, mv[:, u % 2, 0:1],
                                                   mv[:, u % 2, 3:4], ALU.subtract, ALU.mult)
                last.then_inc(tokens_normed, 1)

            def x_rest(u):
                b = bank[7]
                dve.wait_ge(tokens_t_out, u + 1)
                nc.vector.tensor_tensor(xTl[:], b[:, 0:P], xTh[:, 0:P].bitcast(F32), ALU.subtract)
                lo = xTh[64:128, P:2 * P]
                nc.vector.tensor_tensor(lo, b[64:128, P:2 * P], lo.bitcast(F32), ALU.subtract).then_inc(tokens_low, 1)

            def rope(u):
                if u == 0:
                    dve.wait_ge(pool_filled, 1)
                else:
                    dve.wait_ge(queries_rotated, u)
                dve.wait_ge(qk_ready, u + 1)
                for part in range(2):
                    h = slice(HEADS * part, HEADS * part + HEADS)
                    src = bank[6][:, DIM * part:DIM * part + DIM].rearrange("p (g d) -> p g d", d=HD)
                    cos = cn[:, C_COS:C_COS + HD].unsqueeze(1).to_broadcast([P, HEADS, HD])
                    sin = cn[:, C_SIN:C_SIN + HD].unsqueeze(1).to_broadcast([P, HEADS, HD])
                    nc.vector.tensor_tensor(rc[:, h], src, cos, ALU.mult)
                    nc.vector.tensor_tensor(rs[:, h], src, sin, ALU.mult).then_inc(rope_products, 1)

            def rotate_keys(u):
                h = HD // 2
                dve.wait_ge(rope_products, 2 * u + 2)
                if u >= 2:
                    dve.wait_ge(keys_t, u - 1)
                nc.vector.tensor_tensor(k_slots(u)[:, :, :, h:HD], by_parity(rc[:, HEADS:2 * HEADS, h:HD]),
                                        by_parity(rs[:, HEADS:2 * HEADS, 0:h]), ALU.add).then_inc(keys_rotated, 1)

            def softmax_shift(u):
                dve.wait_ge(pool_filled, 2)
                dve.wait_ge(scores_ready, u + 1)
                if u >= 2:
                    dve.wait_ge(probs_t, u - 1)
                s = pso[:, :, 0:4 * SEQ].rearrange("p r (g k) -> p r g k", k=SEQ)
                m = mark(nc.vector.tensor_reduce(mx[:].rearrange("p (r g) -> p r g", r=3), s, AX_X, ALU.max))
                after(m)
                nc.vector.tensor_tensor(
                    pr[:, u % 2].rearrange("p (r e) i k -> p r (e i) k", e=2)[:, :, :, 0:SEQ], s,
                    mx[:].rearrange("p (r g) -> p r g", r=3).unsqueeze(3).to_broadcast([P, 3, 4, SEQ]),
                    ALU.subtract).then_inc(scores_shifted, 1)

            def divide(u, between=None):
                dve.wait_ge(exps_ready, u + 1)
                e = pr[:, u % 2, :, :, 0:SEQ].rearrange("p g i k -> p (g i) k")
                m = mark(nc.vector.tensor_reduce(rec[:, 0, :], e, AX_X, ALU.add))
                if between is not None:
                    between()
                after(m)
                m = mark(nc.vector.reciprocal(rec[:, 1, :], rec[:, 0, :]))
                after(m)
                nc.vector.tensor_tensor(e, e, rec[:, 1, :].unsqueeze(2).to_broadcast([P, HEADS, SEQ]),
                                        ALU.mult).then_inc(probs_ready, 1)

            def last_softmax():
                dve.wait_ge(scores_ready, LAST + 1)
                dve.wait_ge(probs_t, LAST - 1)
                scores_of = [pso[:, r, 0:4 * SEQ].rearrange("p (g k) -> p g k", k=SEQ) for r in range(3)]
                parts = [slice(4 * r, 4 * r + 4) for r in range(3)]
                tops = [mark(nc.vector.tensor_reduce(mx[:, parts[r]], scores_of[r], AX_X, ALU.max)) for r in range(3)]
                for r in range(3):
                    after(tops[r])
                    nc.vector.tensor_tensor(last_probs(r), scores_of[r],
                                            mx[:, parts[r]].unsqueeze(2).to_broadcast([P, 4, SEQ]),
                                            ALU.subtract).then_inc(last_scores_shifted, 1)
                for r in range(3):
                    dve.wait_ge(last_exps_ready, r + 1)
                    m = mark(nc.vector.tensor_reduce(rec[:, 0, parts[r]], last_probs(r), AX_X, ALU.add))
                after(m)
                m = mark(nc.vector.reciprocal(rec[:, 1, :], rec[:, 0, :]))
                after(m)
                for r in range(3):
                    nc.vector.tensor_tensor(last_probs(r), last_probs(r),
                                            rec[:, 1, parts[r]].unsqueeze(2).to_broadcast([P, 4, SEQ]),
                                            ALU.mult).then_inc(last_probs_ready, 1)

            def residual(u):
                t = u % TILES
                dve.wait_ge(projected, u + 1)
                if u >= TILES:
                    dve.wait_ge(bias_added, u - TILES + 1)
                nc.vector.tensor_tensor(hid[:, t, :], hid[:, t, :], bank[4][:, 0:DIM],
                                        ALU.add).then_inc(residual_added, 1)

            def router(u):
                n = u - TILES
                b = u % 2
                lg = hal[:, P:P + EXP]
                iota = cn[:, C_IOTA:C_IOTA + EXP]
                dve.wait_ge(low_rank_ready, n + 1)
                dve.wait_ge(d_lw, 16)
                m = mark(nc.vector.tensor_tensor(hal[:], bank[4][:, 0:P + EXP], lws[:, L_BAR:L_BAR + P + EXP], ALU.add))
                after(m)
                m = mark(nc.vector.max(rt[:, 0, :], lg))
                after(m)
                nc.vector.tensor_scalar(rt[:, 1, :], lg, rt[:, 0, 0:1], None, ALU.subtract).then_inc(logits_shifted, 1)
                m = mark(nc.vector.max_index(rti[:], rt[:, 0, :], lg))
                after(m)
                m = mark(nc.vector.tensor_copy(rt[:, 5, 0:2], rti[:, 0:2]))
                after(m)
                nc.vector.tensor_scalar(rt[:, 6, :], iota, rt[:, 5, 0:1], 2.0, ALU.is_equal, ALU.mult)
                m = mark(nc.vector.tensor_scalar(rt[:, 7, :], iota, rt[:, 5, 1:2], 2.0, ALU.is_equal, ALU.mult))
                dve.wait_ge(router_exps, n + 1)
                mr = mark(nc.vector.reciprocal(rt[:, 3, 1:2], rt[:, 3, 0:1]))
                after(m)
                m = mark(nc.vector.tensor_tensor(rt[:, 4, :], rt[:, 6, :], rt[:, 7, :], ALU.add))
                after(m)
                m = mark(nc.vector.scalar_tensor_tensor(xn[:, b, DIM:DIM + EXP], rt[:, 2, :], rt[:, 3, 1:2], rt[:, 4, :],
                                                        ALU.mult, ALU.mult))
                after(m)
                nc.vector.tensor_tensor(hw[:].rearrange("p (e r) -> p e r", r=RANK),
                                        hal[:, 0:P].rearrange("p (e r) -> p e r", r=RANK),
                                        xn[:, b, DIM:DIM + EXP].unsqueeze(2).to_broadcast([P, EXP, RANK]),
                                        ALU.mult).then_inc(states_scaled, 1)

            def x2_rest(u):
                dve.wait_ge(tokens_high2, u - TILES + 1)
                nc.vector.tensor_tensor(xTl[:], xT[:, 0, :], xTh[:, 0:P].bitcast(F32), ALU.subtract).then_inc(tokens_low2, 1)

            def hw_rest(u):
                dve.wait_ge(states_high, u - TILES + 1)
                nc.vector.tensor_tensor(hwTl[0:KB, P:2 * P], bank[5][0:KB, P:2 * P],
                                        hwTh[0:KB, P:2 * P].bitcast(F32), ALU.subtract)
                nc.vector.tensor_tensor(hwTl[:, 0:P], bank[5][:, 0:P], hwTh[:, 0:P].bitcast(F32),
                                        ALU.subtract).then_inc(states_low, 1)

            token(0)
            stats(0)
            normalise(0)
            x_rest(0)
            for u in range(UNITS + 2):
                a, b = u - 1, u - 2
                layer2 = TILES <= u < UNITS
                if u < TILES:
                    if u >= 3:
                        residual(u - 3)
                    if u + 1 < TILES:
                        token(u + 1)
                    stats(u + 1)
                    if a >= 0:
                        softmax_shift(a)
                    rope(u)
                    normalise(u + 1)
                    rotate_keys(u)
                    if u == 1:
                        embed_low(1)
                    following = (lambda: x_rest(u + 1)) if u + 1 < TILES else None
                    if a >= 0:
                        divide(a, following)
                    elif following:
                        following()
                    continue
                if u == TILES:
                    residual(u - 3)
                if u < UNITS:
                    if u + 1 < UNITS:
                        stats(u + 1)
                    x2_rest(u)
                    router(u)
                    if u + 1 < UNITS:
                        normalise(u + 1)
                if layer2:
                    softmax_shift(a)
                    hw_rest(u)
                    divide(a, lambda: residual(b))
                    continue
                if a == LAST:
                    last_softmax()
                residual(b)

        @block.tensor
        def _(pe):
            xhv = xh[:].rearrange("p c (i r m) -> p c i r m", r=ROWS, m=WINS)
            xlv = xl[:].rearrange("p c (i r m) -> p c i r m", r=ROWS, m=WINS)

            def cells(a):
                i0, i1 = (1, GRID) if a == 0 else (0, GRID - 1) if a == 3 else (0, GRID)
                r0 = 2 * i0 - 1 + a
                return i0, i1, slice(r0, r0 + 2 * (i1 - i0) - 1, 2)

            def moving(v, a, half, ih):
                return v[:, 8 * ih:8 * ih + 8, cells(a)[2], half:half + GRID]

            def patches(b, a):
                i0, i1, _ = cells(a)
                return b[:, 0:HALF].rearrange("p (n i j) -> p n i j", i=GRID, j=GRID)[:, :, i0:i1, :]

            pe.wait_ge(zeros_for_warmup, 1)
            for _ in range(13):
                pe.matmul(bank[7], idle[:, 0:P], idle[:], start=True, stop=True)
            pe.wait_ge(dve_filled, 1)
            pe.wait_ge(d_gb, 16)

            def row_sums(c):
                pe.wait_ge(d_w[c][0], 16)
                pe.wait_ge(d_w[c][1], 16)
                for k in range(10):
                    n = 10 * c + k
                    g = n % 4
                    mm = pe.matmul(bank[4][32 * g:32 * g + 2, 0:DIM], gb[:, n, :], win[:, c, k, :],
                                   start=(n < 4), stop=(n >= CH * 10 - 4), tile_position=(0, 32 * g))
                return mm

            HIGH = ((0, xhv, 0),)
            W_LOW = ((2, xhv, 1), (1, xhv, 0))
            X_LOW = ((0, xlv, 0), (2, xlv, 1))

            def windows(c, k, ih, passes):
                kind, a2, half = k // 4, (k // 2) % 2, k % 2
                a = 1 + a2 if kind == 1 else 3 * a2
                for part, v, b0 in passes:
                    opens = c == 0 and k == 0 and v is xhv and part != 1
                    closes = c == CH - 1 and k == 7 and v is xlv
                    mm = pe.matmul(patches(bank[2 * ih + b0], a), ws[:, c, k, part * P:(part + 1) * P],
                                   moving(v[:, c], a, half, ih), start=opens, stop=closes, skip_group_check=True)
                return mm

            def wait_high(c, part):
                pe.wait_ge(pixels_high, 2 * c + 2)
                pe.wait_ge(weights_high, 2 * c + part + 1)

            def wait_low(c, part):
                pe.wait_ge(pixels_low, 2 * c + 2)
                pe.wait_ge(weights_low, 2 * c + part + 1)

            pe.wait_ge(weights_high, 1)
            for ih in range(2):
                pe.wait_ge(pixels_high, ih + 1)
                for k in range(4):
                    windows(0, k, ih, HIGH)
            pe.wait_ge(weights_low, 1)
            for k in range(4):
                for ih in range(2):
                    windows(0, k, ih, W_LOW)
            row_sums(0)
            for ih in range(2):
                pe.wait_ge(pixels_low, ih + 1)
                for k in range(4):
                    windows(0, k, ih, X_LOW)
            later = [(1, 2), (1, 3), (1, 4), (1, 5), (1, 6), (1, 7)] + [(2, k) for k in range(8)]
            for c in range(2):
                for part in range(2):
                    if (c, part) == (0, 0):
                        continue
                    wait_high(c, part)
                    wait_low(c, part)
                    for k in range(4 * part, 4 * part + 4):
                        for ih in range(2):
                            if ih == 0 or (c, k) not in later:
                                windows(c, k, ih, HIGH + W_LOW + X_LOW)
                mm = row_sums(c + 1)
            mm.then_inc(weight_sums, 1)

            pe.wait_ge(dve_filled, 2)
            pe.wait_ge(channel_sums, 4)
            planes = [v.rearrange("p (i r m) -> p i r m", r=ROWS, m=WINS) for v in (xsum[:], xsq[:, 1])]
            for n, a in enumerate((1, 0, 3, 2)):
                for ih in range(2):
                    for g in range(4):
                        half = g % 2
                        w = C_ONE if a in (0, 3) else C_W0 + half
                        mm = pe.matmul(patches(bank[5 + ih][32 * g:32 * g + 1, :], a), cn[:, w:w + 1],
                                       moving(planes[g // 2], a, half, ih), start=(n == 0), stop=(n == 3),
                                       tile_position=(0, 32 * g))
            mm.then_inc(patch_sums, 1)
            def last_channel(ks):
                for k in ks:
                    wait_high(2, k // 4)
                    wait_low(2, k // 4)
                    mm = windows(2, k, 0, HIGH + W_LOW + X_LOW)
                return mm

            def fill_gap(first, n):
                for c, k in later[first:first + n]:
                    mm = windows(c, k, 1, HIGH + W_LOW + X_LOW)
                if first + n == len(later):
                    mm.then_inc(embed_summed, 1)

            last_channel(range(0, 2))
            pe.wait_ge(d_cn, 16)
            pe.wait_ge(weight_sums_out, 1)
            pe.wait_ge(d_misc, 32)
            pe.matmul(bank[4][:, 0:DIM], cn[:, C_SELW:C_SELW + P], rows[:], start=True, stop=True)
            pe.matmul(bank[4][:, DIM:2 * DIM], cn[:, C_SELB:C_SELB + P], rows[:], start=True, stop=False)
            pe.matmul(bank[4][:, DIM:2 * DIM], brow[:, DIM:DIM + P], brow[:, 0:DIM],
                      start=False, stop=True).then_inc(weight_sums_spread, 1)
            last_channel(range(2, 3))
            pe.wait_ge(patch_sums_out, 2)
            for t in range(TILES):
                mm = pe.matmul(bank[6][:, 2 * t:2 * t + 2], stT[:, t, :], cn[:, C_SELS:C_SELS + 2], start=True, stop=True)
            mm.then_inc(patch_means, 1)
            last_channel(range(3, 8)).then_inc(embed_summed, 1)

            def embed_token(u):
                pe.wait_ge(embed_high_out, 1 + u // 4)
                pe.wait_ge(embed_low_out, 1 + u // 4)
                if u >= 2:
                    pe.wait_ge(queries_t_out, u - 1)
                pe.transpose(bank[5][:, 0:P], eT[:, 0, u, :], ident)
                pe.matmul(bank[5][:, P:DIM], eT[:, 1, u, :], cn[:, C_STACK:C_STACK + 64], start=False, stop=False,
                          skip_group_check=True)
                pe.matmul(bank[5][:, 0:DIM], stT[:, u, :], wmean[:], start=False, stop=True,
                          skip_group_check=True).then_inc(embed_tokens, 1)

            def x_transpose(u):
                pe.wait_ge(tokens_normed, u + 1)
                if u > TILES:
                    pe.wait_ge(residual_added, u - 2)
                elif u >= 1:
                    pe.wait_ge(values_out, u)
                b = x_bank(u)
                pe.transpose(b[:, 0:P], xn[:, u % 2, 0:P], ident)
                if u < TILES:
                    pe.transpose(b[:, P:2 * P], xd[:, u % 2].rearrange("p c n -> p (c n)"), ident).then_inc(tokens_t, 1)
                    return
                pe.transpose(b[0:64, P:2 * P], xn[:, u % 2, P:DIM], ident).then_inc(tokens_t, 1)

            def split_products(to, n):
                first, second = xTh[:, 0:P], xTh[:, P:2 * P]
                pe.matmul(to, first, wTh[:, 0, n], start=True, stop=False)
                pe.matmul(to, xTl[:], wTh[:, 0, n], start=False, stop=False)
                pe.matmul(to, first, wTl[:, 0, n], start=False, stop=False)
                pe.matmul(to, second, wTh[:, 1, n], start=False, stop=False)
                return pe.matmul(to, second[0:64], wTl[0:64, 1, n], start=False, stop=True)

            def qk_rotary(u):
                pe.wait_ge(tokens_low, u + 1)
                if u >= 1:
                    pe.wait_ge(keys_t_out, u)
                else:
                    pe.wait_ge(variances_ready, 1)
                    pe.wait_ge(w1_low, 1)
                split_products(bank[6][:, 0:2 * DIM], slice(0, 2 * DIM)).then_inc(qk_ready, 1)

            def values(u):
                if u >= 1:
                    pe.wait_ge(scores_shifted, u)
                split_products(bank[7][:, 0:DIM], slice(2 * DIM, 3 * DIM)).then_inc(values_ready, 1)

            def low_rank(u):
                pe.wait_ge(tokens_t_out, u + 1)
                w = lws[:, L_AR:L_P2].rearrange("p (k n) -> p k n", k=2)
                if u == TILES:
                    pe.wait_ge(residual_added, u - 2)
                pe.matmul(bank[4][:, 0:P + EXP], xT[:, 0, :], w[:, 0], start=True, stop=False)
                pe.matmul(bank[4][:, 0:P + EXP], xT[0:64, 1, :], w[0:64, 1], start=False,
                          stop=True).then_inc(low_rank_ready, 1)

            def high_part(to, high, k, n, first=False):
                n_rows = high.shape[0]
                pe.matmul(to, high, w2h[0:n_rows, k, n], start=first, stop=False)
                pe.matmul(to, high, w2l[0:n_rows, k, n], start=False, stop=False)

            def low_part(to, low, k, n, last=False):
                return pe.matmul(to, low, w2h[0:low.shape[0], k, n], start=False, stop=last)

            qk_columns, v_columns = slice(0, 2 * DIM), slice(2 * DIM, 3 * DIM)

            def qk_direct(u):
                pe.wait_ge(keys_t_out, u)
                pe.wait_ge(tokens_low2, u - TILES + 1)
                if u == TILES:
                    pe.wait_ge(w2_low, 3)
                to = bank[6][:, 0:2 * DIM]
                high_part(to, xTh[:, 0:P], 0, qk_columns, first=True)
                low_part(to, xTl[:], 0, qk_columns)

            def qkv_experts(u):
                qk, v = bank[6][:, 0:2 * DIM], bank[7][:, 0:DIM]
                pe.wait_ge(states_high, u - TILES + 1)
                high_part(qk, hwTh[0:KB, P:2 * P], 1, qk_columns)
                high_part(qk, hwTh[:, 0:P], 2, qk_columns)
                pe.wait_ge(states_low, u - TILES + 1)
                low_part(qk, hwTl[0:KB, P:2 * P], 1, qk_columns)
                low_part(qk, hwTl[:, 0:P], 2, qk_columns, last=True).then_inc(qk_ready, 1)
                pe.wait_ge(scores_shifted, u)
                high_part(v, xTh[:, 0:P], 0, v_columns, first=True)
                low_part(v, xTl[:], 0, v_columns)
                high_part(v, hwTh[0:KB, P:2 * P], 1, v_columns)
                low_part(v, hwTl[0:KB, P:2 * P], 1, v_columns)
                high_part(v, hwTh[:, 0:P], 2, v_columns)
                low_part(v, hwTl[:, 0:P], 2, v_columns, last=True).then_inc(values_ready, 1)

            def hw_transpose(u):
                pe.wait_ge(states_scaled, u - TILES + 1)
                pe.wait_ge(queries_t_out, u)
                pe.transpose(bank[5][:, 0:P], hw[:], ident)
                pe.transpose(bank[5][0:KB, P:2 * P], xn[:, u % 2, P:LIN], ident).then_inc(states_t, 1)

            def qk_transpose(u):
                if u < TILES:
                    pe.wait_ge(queries_rotated, u + 1)
                    pe.wait_ge(keys_rotated, u + 1)
                else:
                    pe.wait_ge(qk_slots2, u - TILES + 1)
                for b in range(2):
                    mm = pe.transpose(bank[5][0:96, b * P:(b + 1) * P], qr[:, u % 2, 96 * b:96 * b + 96], ident)
                mm.then_inc(queries_t, 1)
                for b in range(4):
                    at = DIM + 96 * b
                    mm = pe.transpose(bank[6][0:96, b * P:(b + 1) * P], qr[:, u % 2, at:at + 96], ident)
                mm.then_inc(keys_t, 1)

            def scores(u):
                pe.wait_ge(queries_t_out, u + 1)
                pe.wait_ge(keys_t_out, u + 1)
                pe.wait_ge(values_out, u + 1)
                if u + 1 < TILES:
                    pe.wait_ge(tokens_low, u + 2)
                elif u + 1 == TILES:
                    pe.wait_ge(tokens_t_out, u + 2)
                if u >= 1:
                    pe.wait_ge(scores_shifted, u)
                else:
                    pe.wait_ge(embed_high_out, 1)
                    pe.wait_ge(embed_low_out, 1)
                masked = u < TILES
                if masked:
                    pe.wait_ge(pool_filled, 6)
                    for r in range(3):
                        pe.matmul(pso[:, r, 0:4 * SEQ], identb, maskb, start=True, stop=True,
                                  skip_group_check=True)
                for n in range(12):
                    r, i, s = n % 3, n // 2 % 2, n % 2
                    to = pso[SLOT * s:SLOT * s + SLOT, r, 0:4 * SEQ].rearrange("p (e i k) -> p e i k", e=2, i=2)
                    mm = pe.matmul(to[:, :, i],
                                   qT[32 * r:32 * r + 32, u % 2, s, SLOT * i:SLOT * i + SLOT],
                                   kT[32 * r:32 * r + 32, u % 2, s:4:2, SLOT * i:SLOT * i + SEQ],
                                   start=not masked, stop=True,
                                   tile_position=(32 * r, SLOT * s), skip_group_check=True)
                mm.then_inc(scores_ready, 1)

            def p_transpose(u, halves=(0, 1)):
                pe.wait_ge(probs_ready, u + 1)
                if u >= 1:
                    pe.wait_ge(attended_out, u)
                else:
                    pe.wait_ge(embed_high_out, 2)
                    pe.wait_ge(embed_low_out, 2)
                for half in halves:
                    for g in range(3):
                        mm = pe.transpose(bank[2 + half][:, g * P:g * P + P],
                                          pr[:, u % 2, 3 * half + g].rearrange("p i k -> p (i k)"), ident)
                if 1 in halves:
                    mm.then_inc(probs_t, 1)

            def attend_block(u, g):
                c, k = g % 4, g // 4
                for s in range(2):
                    for i in range(2):
                        mm = pe.matmul(bank[2 + i][32 * c:32 * c + 32, SLOT * k:SLOT * k + SLOT],
                                       vs[SLOT * i:SLOT * i + SLOT, u % 3, 6 * s + g, :],
                                       pT[SLOT * i:SLOT * i + SLOT, g, s, :],
                                       start=(s == 0), stop=(s == 1), tile_position=(SLOT * i, 32 * c))
                return mm

            def attend(u):
                pe.wait_ge(probs_t_out, u + 1)
                pe.wait_ge(values_out, u + 1)
                for g in range(6):
                    mm = attend_block(u, g)
                mm.then_inc(attended, 1)

            def last_p_transpose():
                for r in range(3):
                    pe.wait_ge(last_probs_ready, r + 1)
                    for e in range(2):
                        mm = pe.transpose(last_pt_banks[r][:, e * P:(e + 1) * P],
                                          pr[:, LAST % 2, 2 * r + e].rearrange("p i k -> p (i k)"), ident)
                    mm.then_inc(last_probs_t, 1)

            def last_attend():
                pe.wait_ge(attended_out, LAST)
                for r in range(3):
                    pe.wait_ge(last_probs_t_out, r + 1)
                    for g in (2 * r, 2 * r + 1):
                        mm = attend_block(LAST, g)
                mm.then_inc(attended, 1)

            def project(u):
                pe.wait_ge(attended_out, u + 1)
                if u >= 1:
                    pe.wait_ge(residual_added, u)
                if TILES <= u + 2 < UNITS:
                    pe.wait_ge(logits_shifted, u + 3 - TILES)
                at = L_O1 if u < TILES else L_P2
                for k, n in ((0, P), (1, 64)):
                    mm = pe.matmul(bank[4][:, 0:DIM], oT[0:n, k, :], lws[0:n, at + k * DIM:at + (k + 1) * DIM],
                                   start=(k == 0), stop=(k == 1))
                mm.then_inc(projected, 1)

            fill_gap(0, 1)
            embed_token(0)
            fill_gap(1, 5)
            x_transpose(0)
            fill_gap(6, 1)
            embed_token(1)
            pe.wait_ge(d_lw, 16)

            def stay_warm(n):
                for _ in range(n):
                    pe.matmul(bank[6][:, 0:4 * SEQ], identb, maskb, start=True, stop=True)

            for u in range(UNITS + 2):
                a, b = u - 1, u - 2
                layer1, layer2 = u < TILES, TILES <= u < UNITS
                if 0 < u < UNITS:
                    x_transpose(u)
                if u == 1:
                    fill_gap(10, 1)
                if 0 <= a < UNITS:
                    qk_transpose(a)
                if u == 1:
                    fill_gap(11, 1)
                if layer1:
                    if u >= 3:
                        project(u - 3)
                    if u >= 1 and u + 1 < TILES:
                        embed_token(u + 1)
                    if a >= 0:
                        scores(a)
                    if b >= 0:
                        p_transpose(b)
                    qk_rotary(u)
                    if u == 1:
                        fill_gap(12, 1)
                    values(u)
                    if u == 0:
                        fill_gap(7, 3)
                    if u == 1:
                        fill_gap(13, 1)
                    if b >= 0:
                        attend(b)
                    continue
                if u == TILES:
                    project(u - 3)
                if b == LAST:
                    stay_warm(1)
                    last_p_transpose()
                    stay_warm(1)
                    last_attend()
                    stay_warm(11)
                    project(b)
                    continue
                p_transpose(b, (0,))
                if layer2:
                    low_rank(u)
                p_transpose(b, (1,))
                scores(a)
                attend(b)
                if a == LAST:
                    stay_warm(14)
                if layer2:
                    hw_transpose(u)
                    qk_direct(u)
                project(b)
                if layer2:
                    qkv_experts(u)


def shape_constants():
    import numpy as np
    c = np.zeros((P, C_N), np.float32)
    tok = np.arange(P) % SLOT
    real = (tok < NPATCH).astype(np.float32)
    c[:, C_ID:C_ID + P] = np.eye(P)
    for g in range(4):
        c[32 * g, C_SELW:C_SELW + P] = 1
        c[32 * g + 1, C_SELB:C_SELB + P] = real
        c[32 * g, C_SELS + g // 2] = 1 / PDIM
    c[0, C_MEAN] = c[32, C_MEAN] = -1 / PDIM
    c[:, C_STACK:C_STACK + 64] = np.tile(np.eye(64), (2, 1))
    pos = np.where(tok < NPATCH, tok + 1, 0).astype(np.float32)
    freq = np.float32(10000.0) ** (-np.arange(0, HD, 2, dtype=np.float32) / HD)
    ang = (pos[:, None] * freq[None, :]).astype(np.float32)
    c[:, C_COS:C_COS + HD] = np.tile(np.cos(ang), (1, 2))
    c[:, C_SIN:C_SIN + HD] = np.tile(np.sin(ang), (1, 2))
    c[:, C_TOK], c[:, C_NTOK], c[:, C_ONE] = real, 1 - real, 1
    right = np.arange(P) >= 64
    c[:, C_W0], c[:, C_W1] = 1 + right, 2 - right
    c[:, C_IOTA:C_IOTA + EXP] = np.arange(EXP)
    c[:, C_HALF:C_HALF + TILES] = -0.5
    place = np.r_[np.arange(1, SEQ), 0]
    hidden = np.where(place[None, :] > place[:, None], np.float32(-1e30), np.float32(0))
    for s in range(2):
        c[SLOT * s:SLOT * s + SEQ, C_MASK:C_N] = np.tile(hidden, (1, 4))
    return c


def kernel(**inputs):
    import numpy as np
    import concourse.bacc as bacc
    from concourse.bass_utils import run_bass_kernel_spmd

    a = {k: np.asarray(v) for k, v in inputs.items()}
    x = a["x"].reshape(IMG, CH, ROWS, 8, GRID, 2, 8)
    xp = np.zeros((2, 8, 8, CH, IMG, ROWS, WINS), np.float32)
    xp[1, :, :, :, :, :, 0:GRID] = x[:, :, :, :, :, 0].transpose(3, 5, 1, 0, 2, 4)
    xp[0, :, :, :, :, :, 1:WINS] = x[:, :, :, :, :, 1].transpose(3, 5, 1, 0, 2, 4)
    xp = xp.reshape(P, CH, IMG * ROWS * WINS)

    def tok_tiles(w):
        w = w.reshape(-1, 2, 8, 16, 5, CH)
        t = np.zeros((2, 8, 8, CH, 10, w.shape[0]), np.float32)
        copy = {(0, 0): 1, (1, 1): 2, (0, 1): 3, (1, 0): 4}
        for k in range(8):
            kind, a2, half = k // 4, (k // 2) % 2, k % 2
            row = 1 + a2 if kind == 1 else 3 * a2
            s = w[:, row % 2, :, :, copy[(row // 2, half)], :].reshape(-1, 8, 2, 8, CH)
            t[:, :, :, :, k] = s.transpose(2, 1, 3, 4, 0)
        for a2 in range(2):
            s = w[:, a2, :, :, 0, :].reshape(-1, 8, 2, 8, CH).transpose(2, 1, 3, 4, 0)
            t[1, :, :, :, 8 + a2], t[0, :, :, :, 8 + a2] = s[0], s[1]
        return t.reshape(P, CH, 10, -1)

    tokw = tok_tiles(a["L0_tok_W"])
    tokgb = tok_tiles(np.stack([a["L0_tok_ln_gamma"], a["L0_tok_ln_beta"]])).reshape(P, CH * 10, 2)
    cls = np.zeros((P, 2), np.float32)
    cls[:, 0] = a["cls_tok"].reshape(DIM)[:P]
    cls[:DIM - P, 1] = a["cls_tok"].reshape(DIM)[P:]

    lnb = np.zeros((1, DIM + P), np.float32)
    lnb[0, :DIM] = a["L0_tok_b"]
    lnb[0, DIM:] = np.arange(P) % SLOT < NPATCH

    lw = np.zeros((P, L_N), np.float32)

    def put(at, w):
        n = w.shape[1]
        lw[:, at:at + n] = w[:P]
        lw[:w.shape[0] - P, at + n:at + 2 * n] = w[P:]

    halves = np.r_[np.arange(0, HD, 2), np.arange(1, HD, 2)]
    wq, wk = (a[f"L0_attn_{n}"].reshape(HEADS, HD, DIM)[:, halves].reshape(DIM, DIM) for n in ("wq", "wk"))
    put(L_QKV1, np.concatenate([wq, wk, a["L0_attn_wv"]]).T)
    lw[64:, L_QKV1 + 3 * DIM:L_O1] = lw[:64, L_QKV1 + 3 * DIM:L_O1]
    wqkv = np.concatenate([a["L0_ffn_Wqkv"].T, a["L0_ffn_bb"], a["L0_ffn_bqkv"][None]])
    put(L_QKV2, wqkv)
    lw[:, L_QKV2 + 6 * DIM:L_AR] = a["L0_ffn_Bm"].transpose(0, 2, 1).reshape(EXP * RANK, 3 * DIM)
    put(L_AR, np.concatenate([a["L0_ffn_A"].reshape(EXP * RANK, DIM), a["L0_ffn_Wg"]]).T)
    for at, w in ((L_O1, a["L0_attn_wo"]), (L_P2, a["L0_ffn_Wproj"])):
        put(at, w.T.reshape(2, 6, HD, DIM).transpose(1, 0, 2, 3).reshape(DIM, DIM))
    lw[:, L_BAR:L_BAR + P] = a["L0_ffn_ba"].reshape(1, -1)
    lw[:, L_BAR + P:L_BP] = a["L0_ffn_bg"][None]
    lw[:, L_BP:L_N] = a["L0_ffn_bproj"][None]

    arrays = {"in_x": xp, "in_tokw": tokw, "in_tokgb": tokgb, "in_b": lnb, "in_cls": cls,
              "in_lw": lw, "in_con": shape_constants()}
    arrays = {k: np.ascontiguousarray(v) for k, v in arrays.items()}
    nc = bacc.Bacc("TRN2", target_bir_lowering=False, num_devices=1)
    args = [nc.dram_tensor(k, v.shape, mybir.dt.from_np(v.dtype), kind="ExternalInput").ap() for k, v in arrays.items()]
    out = nc.dram_tensor("out", (TILES, P, DIM), F32, kind="ExternalOutput").ap()
    vit_tower(nc, *args, out)
    got = run_bass_kernel_spmd(nc, [arrays], core_ids=[0]).results[0]["out"]
    got = got.reshape(IMG, SLOT, DIM)
    return np.concatenate([got[:, NPATCH:SEQ], got[:, 0:NPATCH]], axis=1)
```
